# Optimizing a Trainium2 kernel written in Bass

```python
import numpy as np
import jax
import jax.numpy as jnp

def _softmax(x, axis=-1):
    return jax.nn.softmax(x, axis=axis)

def _gelu(x):
    return jax.nn.gelu(x, approximate=True)

def _silu(x):
    return jax.nn.silu(x)

def _sigmoid(x):
    return jax.nn.sigmoid(x)

def _layernorm(x, axis=-1, eps=1e-05):
    m = jnp.mean(x, axis=axis, keepdims=True)
    v = jnp.var(x, axis=axis, keepdims=True)
    return (x - m) / jnp.sqrt(v + eps)

def _scatter_add(tgt, idx, src, axis=0):
    return tgt.at[idx].add(src)

def _segment_sum(src, seg, n):
    return jax.ops.segment_sum(src, seg, n)
kernel_name = 'mk_sandwich_d1_jaxref_r8_2d8a92'

def setup_inputs(seed: int=0):
    np.random.seed(seed)
    _w = jnp.asarray

    def _L0_attn_setup():
        import jax, jax.numpy as jnp
        import numpy as np
        B, L, D = (2, 256, 128)
        H, K = (16, 16)
        HD = D // H

        def tisa_bias(offsets, amplitudes, sharpness, seq_len):
            rel = jnp.arange(-(seq_len - 1), seq_len, dtype=jnp.float32)
            diff = offsets[:, :, None] - rel[None, None, :]
            scores = jnp.sum(amplitudes[:, :, None] * jnp.exp(-jnp.abs(sharpness)[:, :, None] * diff * diff), axis=1)
            i = jnp.arange(seq_len)
            idx = i[:, None] - i[None, :] + (seq_len - 1)
            return scores[:, idx]
        key = jax.random.key(seed)
        k1, k2, k3, k4, k5 = jax.random.split(key, 5)
        x = jax.random.normal(k1, (B, L, D), dtype=jnp.float32)
        w_in = jax.random.normal(k2, (3 * D, D), dtype=jnp.float32) * 0.02
        kernel_offsets = jax.random.normal(k3, (H, K), dtype=jnp.float32) * 20.0
        kernel_amplitudes = 0.1 + 0.01 * jax.random.normal(k4, (H, K), dtype=jnp.float32)
        kernel_sharpness = 0.1 + 0.01 * jax.random.normal(k5, (H, K), dtype=jnp.float32)
        return {'x': x, 'w_in': w_in, 'kernel_offsets': kernel_offsets, 'kernel_amplitudes': kernel_amplitudes, 'kernel_sharpness': kernel_sharpness}
    _L0_attn_in = _L0_attn_setup()

    def _L0_ffn_setup():
        import jax, jax.numpy as jnp
        import numpy as np
        B, N, D, H, E = (4, 128, 128, 16, 8)
        DK = D // H
        HID = 4 * D
        EPS = 1e-05

        def _layernorm(x, w, b):
            m = jnp.mean(x, axis=-1, keepdims=True)
            v = jnp.mean(jnp.square(x - m), axis=-1, keepdims=True)
            return (x - m) * jax.lax.rsqrt(v + EPS) * w + b

        def _msa(x, w_qkv, w_proj):
            b, n, d = x.shape
            qkv = (x @ w_qkv).reshape(b, n, 3, H, DK)
            q = qkv[:, :, 0].transpose(0, 2, 1, 3)
            k = qkv[:, :, 1].transpose(0, 2, 1, 3)
            v = qkv[:, :, 2].transpose(0, 2, 1, 3)
            attn = jnp.einsum('bhnd,bhmd->bhnm', q, k) * (1.0 / np.sqrt(DK))
            attn = jax.nn.softmax(attn, axis=-1)
            y = jnp.einsum('bhnm,bhmd->bhnd', attn, v)
            y = y.transpose(0, 2, 1, 3).reshape(b, n, d)
            return y @ w_proj

        def _moe_mlp(x, gate_w, gate_b, w1, w2):
            b, n, d = x.shape
            xf = x.reshape(b * n, d)
            logits = xf @ gate_w + gate_b
            one_hot = jax.nn.one_hot(jnp.argmax(logits, axis=-1), E, dtype=xf.dtype)
            h = jax.nn.gelu(jnp.einsum('td,edh->teh', xf, w1), approximate=True)
            y = jnp.einsum('teh,ehd->ted', h, w2)
            out = jnp.einsum('te,ted->td', one_hot, y)
            return out.reshape(b, n, d)
        key = jax.random.key(seed)
        ks = jax.random.split(key, 8)
        s = 0.02
        return {'x': jax.random.normal(ks[0], (B, N, D), jnp.float32), 'ln1_w': jnp.ones((D,), jnp.float32), 'ln1_b': jnp.zeros((D,), jnp.float32), 'w_qkv': jax.random.normal(ks[1], (D, 3 * D), jnp.float32) * s, 'w_proj': jax.random.normal(ks[2], (D, D), jnp.float32) * s, 'ln2_w': jnp.ones((D,), jnp.float32), 'ln2_b': jnp.zeros((D,), jnp.float32), 'gate_w': jax.random.normal(ks[3], (D, E), jnp.float32) * s, 'gate_b': jnp.zeros((E,), jnp.float32), 'w1': jax.random.normal(ks[4], (E, D, HID), jnp.float32) * s, 'w2': jax.random.normal(ks[5], (E, HID, D), jnp.float32) * s}
    _L0_ffn_in = _L0_ffn_setup()
    _d = {'L0_attn_x': _L0_attn_in['x'], 'L0_attn_w_in': _L0_attn_in['w_in'], 'L0_attn_kernel_offsets': _L0_attn_in['kernel_offsets'], 'L0_attn_kernel_amplitudes': _L0_attn_in['kernel_amplitudes'], 'L0_attn_kernel_sharpness': _L0_attn_in['kernel_sharpness'], 'L0_ffn_ln1_w': _L0_ffn_in['ln1_w'], 'L0_ffn_ln1_b': _L0_ffn_in['ln1_b'], 'L0_ffn_w_qkv': _L0_ffn_in['w_qkv'], 'L0_ffn_w_proj': _L0_ffn_in['w_proj'], 'L0_ffn_ln2_w': _L0_ffn_in['ln2_w'], 'L0_ffn_ln2_b': _L0_ffn_in['ln2_b'], 'L0_ffn_gate_w': _L0_ffn_in['gate_w'], 'L0_ffn_gate_b': _L0_ffn_in['gate_b'], 'L0_ffn_w1': _L0_ffn_in['w1'], 'L0_ffn_w2': _L0_ffn_in['w2']}
    _x0 = _d['L0_attn_x']
    _d['L0_attn_x'] = jax.random.normal(jax.random.fold_in(jax.random.key(seed), 1), (2, 1024, 128), dtype=_x0.dtype)
    del _x0
    return _d

def reference(L0_attn_x, L0_attn_w_in, L0_attn_kernel_offsets, L0_attn_kernel_amplitudes, L0_attn_kernel_sharpness, L0_ffn_ln1_w, L0_ffn_ln1_b, L0_ffn_w_qkv, L0_ffn_w_proj, L0_ffn_ln2_w, L0_ffn_ln2_b, L0_ffn_gate_w, L0_ffn_gate_b, L0_ffn_w1, L0_ffn_w2):

    def _L0_attn_ref(x, w_in, kernel_offsets, kernel_amplitudes, kernel_sharpness):
        import jax, jax.numpy as jnp
        import numpy as np
        B, L, D = (2, 256, 128)
        H, K = (16, 16)
        HD = D // H

        def tisa_bias(offsets, amplitudes, sharpness, seq_len):
            rel = jnp.arange(-(seq_len - 1), seq_len, dtype=jnp.float32)
            diff = offsets[:, :, None] - rel[None, None, :]
            scores = jnp.sum(amplitudes[:, :, None] * jnp.exp(-jnp.abs(sharpness)[:, :, None] * diff * diff), axis=1)
            i = jnp.arange(seq_len)
            idx = i[:, None] - i[None, :] + (seq_len - 1)
            return scores[:, idx]
        b, l, d = x.shape
        proj = jnp.einsum('bld,ed->ble', x, w_in)
        k_, v_, q_ = (proj[..., :d], proj[..., d:2 * d], proj[..., 2 * d:])

        def heads(t):
            return t.reshape(b, l, H, HD).transpose(0, 2, 1, 3)
        q, k, v = (heads(q_), heads(k_), heads(v_))
        bias = tisa_bias(kernel_offsets, kernel_amplitudes, kernel_sharpness, l)
        scale = 1.0 / np.sqrt(HD).astype(np.float32)
        logits = jnp.einsum('bhld,bhmd->bhlm', q, k) * scale + bias[None]
        attn = jax.nn.softmax(logits, axis=-1)
        out = jnp.einsum('bhlm,bhmd->bhld', attn, v)
        return out.transpose(0, 2, 1, 3).reshape(b, l, d)

    def _L0_ffn_ref(x, ln1_w, ln1_b, w_qkv, w_proj, ln2_w, ln2_b, gate_w, gate_b, w1, w2):
        import jax, jax.numpy as jnp
        import numpy as np
        B, N, D, H, E = (4, 128, 128, 16, 8)
        DK = D // H
        HID = 4 * D
        EPS = 1e-05

        def _layernorm(x, w, b):
            m = jnp.mean(x, axis=-1, keepdims=True)
            v = jnp.mean(jnp.square(x - m), axis=-1, keepdims=True)
            return (x - m) * jax.lax.rsqrt(v + EPS) * w + b

        def _msa(x, w_qkv, w_proj):
            b, n, d = x.shape
            qkv = (x @ w_qkv).reshape(b, n, 3, H, DK)
            q = qkv[:, :, 0].transpose(0, 2, 1, 3)
            k = qkv[:, :, 1].transpose(0, 2, 1, 3)
            v = qkv[:, :, 2].transpose(0, 2, 1, 3)
            attn = jnp.einsum('bhnd,bhmd->bhnm', q, k) * (1.0 / np.sqrt(DK))
            attn = jax.nn.softmax(attn, axis=-1)
            y = jnp.einsum('bhnm,bhmd->bhnd', attn, v)
            y = y.transpose(0, 2, 1, 3).reshape(b, n, d)
            return y @ w_proj

        def _moe_mlp(x, gate_w, gate_b, w1, w2):
            b, n, d = x.shape
            xf = x.reshape(b * n, d)
            logits = xf @ gate_w + gate_b
            one_hot = jax.nn.one_hot(jnp.argmax(logits, axis=-1), E, dtype=xf.dtype)
            h = jax.nn.gelu(jnp.einsum('td,edh->teh', xf, w1), approximate=True)
            y = jnp.einsum('teh,ehd->ted', h, w2)
            out = jnp.einsum('te,ted->td', one_hot, y)
            return out.reshape(b, n, d)
        x = x + _msa(_layernorm(x, ln1_w, ln1_b), w_qkv, w_proj)
        x = x + _moe_mlp(_layernorm(x, ln2_w, ln2_b), gate_w, gate_b, w1, w2)
        return x
    x = L0_attn_x
    x = x + _layernorm(_L0_attn_ref(_layernorm(x, axis=-1), L0_attn_w_in, L0_attn_kernel_offsets, L0_attn_kernel_amplitudes, L0_attn_kernel_sharpness), axis=-1)
    x = x + _layernorm(_L0_ffn_ref(_layernorm(x, axis=-1), L0_ffn_ln1_w, L0_ffn_ln1_b, L0_ffn_w_qkv, L0_ffn_w_proj, L0_ffn_ln2_w, L0_ffn_ln2_b, L0_ffn_gate_w, L0_ffn_gate_b, L0_ffn_w1, L0_ffn_w2), axis=-1)
    return x

_drawn_inputs = setup_inputs


def setup_inputs(seed=0):
    import zlib

    import numpy as np

    out = dict(_drawn_inputs(seed))
    spreads = {'L0_ffn_ln1_w': (1.0, 0.6),
     'L0_ffn_ln1_b': (0.0, 0.8),
     'L0_ffn_ln2_w': (1.0, 0.6),
     'L0_ffn_ln2_b': (0.0, 2.0),
     'L0_ffn_gate_b': (0.0, 1.497)}
    factors = {'L0_attn_kernel_offsets': 3.001,
     'L0_attn_kernel_amplitudes': 28.391,
     'L0_attn_kernel_sharpness': 64.0,
     'L0_ffn_w_qkv': 3.438,
     'L0_ffn_w_proj': 3.512,
     'L0_ffn_gate_w': 2.8}
    for name, (base, spread) in spreads.items():
        noise = np.random.default_rng([zlib.crc32(name.encode()), seed]).standard_normal(out[name].shape)
        drawn = base * np.exp(spread * noise) if base else spread * noise
        out[name] = jnp.asarray(drawn.astype(out[name].dtype))
    for name, factor in factors.items():
        out[name] = (out[name] * factor).astype(out[name].dtype)
    return out
```

```python
import concourse.bass as bass
from concourse import mybir
from contextlib import ExitStack
import numpy as np


def sandwich_kernel(nc, x, w_in, offsets, amplitudes, sharpness, ln1_w, ln1_b, w_qkv, w_proj,
                    ln2_w, ln2_b, gate_w, gate_b, w1, w2, out):
    fp32, bf16 = mybir.dt.float32, mybir.dt.bfloat16
    ALU, ACT, AX = mybir.AluOpType, mybir.ActivationFunctionType, mybir.AxisListType

    B, L, D = x.shape
    P = 128
    T = B * L
    TT = T // P
    H = offsets.shape[0]
    NK = offsets.shape[1]
    DH = D // H
    SCALE = float(np.float32(1.0) / np.sqrt(np.float32(DH)))
    EPS = 1e-5
    E, _, HID = w1.shape
    HC = HID // P
    U = B * H
    QB = L // P
    N = 512
    G = T // N
    TG = N // P
    LEAST = -3.0e38
    PAIRS = H // 2
    RUNS = [(0, 3, 0), (3, 2, 1), (5, 1, 2)]
    KR = 6 * DH
    QK_DMAS = 2 * len(RUNS)
    REL = 2 * L - 1
    TAW = 2 * L - P
    VM = 32

    parts_dram = [nc.dram_tensor(f"parts{a}", (2, 3, D, T), bf16, kind="Internal").ap() for a in range(2)]
    heads_dram = [nc.dram_tensor(f"heads{a}", (U, P, L // 4), fp32, kind="Internal").ap() for a in range(2)]
    maxima_dram = nc.dram_tensor("maxima_rows", (2, 3 * QB, P), bf16, kind="Internal").ap()
    bias_dram = nc.dram_tensor("bias_rows", (H, 2 * L), fp32, kind="Internal").ap()

    with ExitStack() as ctx:
        def sb(name, shape, dt=fp32):
            return ctx.enter_context(nc.sbuf_tensor(name, shape, dt))

        def sem(name):
            return ctx.enter_context(nc.semaphore(name))

        x_res = sb("x_res", [P, TT, D])
        y_res = sb("y_res", [P, TT, D])
        norm = sb("norm", [P, TT, D])
        feat = sb("feat", [P, T])
        v_nat = sb("v_nat", [P, TT, D])
        sums = v_nat[0:H].rearrange("p t d -> p (t d)")
        q_rows = sb("q_rows", [P, 2, T], bf16)
        k_rows = sb("k_rows", [P, 2, T], bf16)
        tables = sb("tables", [P, 4096])
        bias_tab = tables[:, 0:2 * TAW].rearrange("p (s c) -> p s c", s=2)
        qb_rows = tables[:, 0:T].bitcast(bf16).rearrange("p (s n) -> p s n", s=2)
        kb_rows = tables[:, T:2 * T].bitcast(bf16).rearrange("p (s n) -> p s n", s=2)
        NT = 4
        logit = sb("logit", [P, NT, L])
        prob_mem = sb("prob_mem", [P, 2 * QB * L])
        prob = prob_mem[:, :].rearrange("p (s k q) -> p s k q", s=2, k=QB)
        bias_e = prob_mem[:, 0:4096].rearrange("p (t n) -> p t n", t=2)
        rel_pos = prob_mem[:, 4096:6144]
        bias_row = prob_mem[0:H, 6144:8192]
        parts = prob_mem[:, 8192:14336].bitcast(bf16).rearrange("p (s t n) -> p s t n", s=2, t=3)
        rest = prob_mem[:, 14336:15360].rearrange("p (s n) -> p s n", s=2)
        hidden = prob_mem[:, 0:2 * HC * N].rearrange("p (r c n) -> p r c n", r=2, c=HC)
        v_ring = sb("v_ring", [P, 2, TT, VM])
        o_ring = sb("o_ring", [P, 2, L // 4])
        w_in_nat = sb("w_in_nat", [P, 3, D])
        w_in_t = sb("w_in_t", [P, 3, D])
        w_qkv_sb = sb("w_qkv_sb", [P, 3, D])
        w_proj_sb = sb("w_proj_sb", [P, D])
        gate_w_sb = sb("gate_w_sb", [P, E])
        gate_b_sb = sb("gate_b_sb", [P, E])
        w1_sb = sb("w1_sb", [P, E, HID])
        w2_sb = sb("w2_sb", [P, E, HC, D])
        ln_par = sb("ln_par", [P, 4])
        bias_par = sb("bias_par", [P, 3, 2])
        neg_sharp = sb("neg_sharp", [P, 2])
        amp_sel = sb("amp_sel", [P, 2, H])
        ident = sb("ident", [P, P])
        ident_b = sb("ident_b", [P, P], bf16)
        head_sel = sb("head_sel", [H, D])
        eps_col = sb("eps_col", [P, 1])
        order = sb("order", [P, E])
        stats = sb("stats", [P, TT, 6])
        meanvar = sb("meanvar", [P, TT, 2])
        std = sb("std", [P, TT])
        rstd = sb("rstd", [P, TT])
        row_max = sb("row_max", [P, QB])
        unit_max = sb("unit_max", [P, 2, QB])
        max_rest = sb("max_rest", [P, 2, 2, QB])
        max_parts = sb("max_parts", [P, 2, 3 * QB], bf16)
        max_rows = sb("max_rows", [3 * QB, 2, P], bf16)
        gate = sb("gate", [P, TT, E])
        gate_max = sb("gate_max", [P, TT, 1])
        onehot = sb("onehot", [P, TT, E])

        bank = ctx.enter_context(nc.psum_tensor("bank", [P, 8, N], fp32))
        SA = [bank[:, 0:2, :], bank[:, 2:4, :]]
        SB = [bank[:, 4, :], bank[:, 5, :]]
        AV = [bank[:, 6, :], bank[:, 7, :]]

        def bcast(ap, n):
            return bass.AP(ap.tensor, ap.offset, [list(s) for s in ap.ap][:-1] + [[0, n]])

        x_loaded = [sem(f"x_loaded{g}") for g in range(G)]
        bias_loaded = sem("bias_loaded")
        weights_loaded = sem("weights_loaded")
        moe_loaded = sem("moe_loaded")
        consts_ready = sem("consts_ready")
        pool_step = sem("pool_step")
        ones_ready = sem("ones_ready")
        sharp_ready = sem("sharp_ready")
        amp_ready = sem("amp_ready")
        bias_sq = sem("bias_sq")
        bias_exp = sem("bias_exp")
        bias_mm = sem("bias_mm")
        bias_out = sem("bias_out")
        bias_stored = sem("bias_stored")
        w_t_mm = sem("w_t_mm")
        w_t_ready = sem("w_t_ready")
        ln_stats = [sem(f"ln{n}_stats") for n in range(6)]
        ln_aggr = [sem(f"ln{n}_aggr") for n in range(6)]
        ln_std = [sem(f"ln{n}_std") for n in range(6)]
        ln_rstd = [sem(f"ln{n}_rstd") for n in range(6)]
        ln_out = [sem(f"ln{n}_out") for n in range(6)]
        tp_done = [sem(f"tp{a}_done") for a in range(3)]
        feat_ready = [sem(f"feat{a}_ready") for a in range(3)]
        q_mm = [sem(f"q{a}_mm") for a in range(2)]
        k_mm = [sem(f"k{a}_mm") for a in range(2)]
        v_mm = [sem(f"v{a}_mm") for a in range(2)]
        part_hi = [sem(f"part{a}_hi") for a in range(2)]
        part_rest = [sem(f"part{a}_rest") for a in range(2)]
        part_mid = [sem(f"part{a}_mid") for a in range(2)]
        part_lo = [sem(f"part{a}_lo") for a in range(2)]
        v_evac = [sem(f"v{a}_evac") for a in range(2)]
        parts_stored = [sem(f"parts{a}_stored") for a in range(2)]
        qk_loaded = [[sem(f"qk{a}_loaded{s}") for s in range(2)] for a in range(2)]
        qkb_loaded = [sem(f"qkb_loaded{s}") for s in range(2)]
        kb_minus = sem("kb_minus")
        tab_loaded = [sem(f"tab_loaded{s}") for s in range(2)]
        sa_done = [sem(f"sa{a}_done") for a in range(2)]
        max_done = [sem(f"max{a}_done") for a in range(2)]
        shift_dve = sem("shift_dve")
        shift_act = sem("shift_act")
        shift_pool = sem("shift_pool")
        sb_done = [sem(f"sb{a}_done") for a in range(2)]
        exp_done = [sem(f"exp{a}_done") for a in range(2)]
        v_ready = [sem(f"v{a}_ready") for a in range(2)]
        av_done = [sem(f"av{a}_done") for a in range(2)]
        o_ready = [sem(f"o{a}_ready") for a in range(2)]
        o_stored = [[sem(f"o{a}_stored{s}") for s in range(2)] for a in range(2)]
        split_step = sem("split_step")
        mrow_stored = sem("mrow_stored")
        mrow_loaded = [sem(f"mrow_loaded{s}") for s in range(2)]
        sums_loaded = [sem(f"sums{a}_loaded") for a in range(2)]
        heads_loaded = [[sem(f"heads{a}_loaded{g}") for g in range(G)] for a in range(2)]
        recip_done = [sem(f"recip{a}_done") for a in range(2)]
        spread_mm = [sem(f"spread{a}_mm") for a in range(2)]
        heads_scaled = [sem(f"heads{a}_scaled") for a in range(2)]
        nat_mm = [sem(f"nat{a}_mm") for a in range(2)]
        nat_ready = [sem(f"nat{a}_ready") for a in range(2)]
        x_added = sem("x_added")
        gate_mm = sem("gate_mm")
        gate_step = sem("gate_step")
        hid_mm = sem("hid_mm")
        hid_ready = sem("hid_ready")
        moe_mm = sem("moe_mm")
        moe_added = sem("moe_added")
        out_ready = sem("out_ready")
        out_stored = sem("out_stored")
        past_wait_dve = sem("past_wait_dve")
        past_wait_pool = sem("past_wait_pool")

        SHIFT_BY = "ADADADAD"
        shift_sem = {"D": shift_dve, "A": shift_act, "P": shift_pool}

        def shift_count(i, l):
            who = SHIFT_BY[l % QB]
            per_body = 4 * SHIFT_BY.count(who)
            return i * per_body + sum(SHIFT_BY[m % QB] == who for m in range(l + 1))

        def use_of_block(u, qb):
            return u * (QB + 1) - 1 + (qb if qb < 3 else qb + 1)

        def use_of_maxima(u):
            return (u + 1) * (QB + 1) + 2

        LAST_MAXIMA = use_of_block(U, 0)
        AU = 2

        ctx.enter_context(nc.allow_non_contiguous_dma(reason="head rows and skewed tables"))
        block = ctx.enter_context(nc.Block())

        @block.sync
        def _(sp):
            for n, v in enumerate((offsets, amplitudes, sharpness)):
                sp.dma_start(bias_par[:, n, :], v.rearrange("(t h) k -> (h k) t", t=2)).then_inc(bias_loaded, 16)
            x_tiles = x.rearrange("b (t p) d -> p (b t) d", p=P)
            for g in range(G):
                sp.dma_start(x_res[:, g * TG:(g + 1) * TG, :], x_tiles[:, g * TG:(g + 1) * TG, :]).then_inc(x_loaded[g], 16)
            sp.dma_start(w_in_nat[:], w_in.rearrange("(c p) d -> p c d", p=P)).then_inc(weights_loaded, 16)
            sp.dma_start(w_qkv_sb[:], w_qkv.rearrange("d (c n) -> d c n", c=3)).then_inc(weights_loaded, 16)
            sp.dma_start(w_proj_sb[:], w_proj).then_inc(weights_loaded, 16)
            sp.dma_start(gate_w_sb[:], gate_w).then_inc(weights_loaded, 16)
            sp.dma_start(gate_b_sb[:], bass.AP(gate_b.tensor, gate_b.offset, [[0, P], [1, E]])).then_inc(weights_loaded, 16)
            for n, v in enumerate((ln1_w, ln1_b, ln2_w, ln2_b)):
                sp.dma_start(ln_par[:, n:n + 1], v.rearrange("(d o) -> d o", o=1)).then_inc(weights_loaded, 16)
            sp.wait_ge(bias_out, 4)
            sp.dma_start(bias_dram, bias_row).then_inc(bias_stored, 16)

            def store_parts(a):
                for g in range(G):
                    for s in range(2):
                        sp.wait_ge(part_lo[a], 2 * g + s + 1)
                        sp.dma_start(parts_dram[a][s, :, :, g * N:(g + 1) * N].rearrange("t p n -> p t n"),
                                     parts[:, s, :, g * N:(g + 1) * N]).then_inc(parts_stored[a], 16)
                sp.wait_ge(parts_stored[a], 16 * 2 * G)

            def rows_of(a, h, slot, q_dst, k_dst, loaded):
                for row, n, k_part in RUNS:
                    at = slice(row * DH, (row + n) * DH)
                    sp.dma_start(q_dst[at, slot, :],
                                 parts_dram[a][0, 0:n, bass.ds(h * DH, DH), :]).then_inc(loaded[slot], 16)
                    k_src = parts_dram[a][1, k_part, bass.ds(h * DH, DH), :]
                    sp.dma_start(k_dst[at, slot, :],
                                 bass.AP(k_src.tensor, k_src.offset, [[0, n], [T, DH], [1, T]])).then_inc(loaded[slot], 16)

            def table_of(h, slot):
                row = bias_dram[bass.ds(h, 1), 0:TAW]
                src = bass.AP(row.tensor, row.offset, [[1, P], [1, TAW]])
                sp.dma_start(bias_tab[:, slot, :], src).then_inc(tab_loaded[slot], 16)

            def store_unit(a, u, slot):
                sp.wait_ge(o_ready[a], u + 1)
                sp.dma_start(heads_dram[a][bass.ds(u, 1)].rearrange("o p n -> (o p) n"),
                             o_ring[:, slot, :]).then_inc(o_stored[a][slot], 16)

            def load_heads(a):
                for s in range(2):
                    sp.wait_ge(o_stored[a][s], 16 * (U // 2))
                src = heads_dram[a].rearrange("(h b) (c r) n -> h b c r n", b=B, c=4)
                dst = feat[:, :].rearrange("p (b c n) -> p b c n", b=B, c=4)
                sdst = sums[:, :].rearrange("p (b c n) -> p b c n", b=B, c=4)
                for b in range(B):
                    sp.dma_start(sdst[:, b], src[:, b, :, DH, :]).then_inc(sums_loaded[a], 16)
                for b in range(B):
                    for c in range(4):
                        sp.dma_start(dst[:, b, c], src[:, b, c, 0:DH, :]).then_inc(heads_loaded[a][b * 2 + c // 2], 16)

            store_parts(0)
            sp.wait_ge(bias_stored, 16)
            sp.wait_ge(ones_ready, 1)
            for h in range(2):
                rows_of(0, h, h, q_rows, k_rows, qk_loaded[0])
                table_of(h, h)
            sp.dma_start(w1_sb[:], w1.rearrange("e d n -> d e n")).then_inc(moe_loaded, 16)
            sp.dma_start(w2_sb[:], w2.rearrange("e (c p) d -> p e c d", p=P)).then_inc(moe_loaded, 16)

            def pair1(i, first=False, last=False):
                for hl in range(2):
                    h = 2 * i + hl
                    if not (first and hl == 0):
                        for b in range(B):
                            store_unit(0, 2 * h - 2 + b, b)
                    if not last:
                        sp.wait_ge(sa_done[0], QB * B * (h + 1))
                        rows_of(0, h + 2, hl, q_rows, k_rows, qk_loaded[0])
                        sp.wait_ge(max_done[0], QB * B * (h + 1))
                        table_of(h + 2, hl)

            pair1(0, first=True)
            with sp.Fori(1, PAIRS - 1) as i:
                pair1(i)
            pair1(PAIRS - 1, last=True)
            for b in range(B):
                store_unit(0, U - 2 + b, b)
            load_heads(0)

            store_parts(1)
            sp.wait_ge(kb_minus, 4)
            for h in range(2):
                rows_of(1, h, h, q_rows, k_rows, qk_loaded[1])
            for h in range(2):
                rows_of(1, h, h, qb_rows, kb_rows, qkb_loaded)

            def maxima_of(u, slot, use, count_first=False):
                sp.wait_ge(max_done[1], use + 1)
                head_slot, b = (slot // B) % 2, slot % B
                sp.dma_start(maxima_dram[slot % 2], max_rows[:, slot % 2, :]).then_inc(mrow_stored, 16)
                sp.wait_ge(mrow_stored, 16 * (u + 1))
                sp.dma_start(qb_rows[KR:KR + 3, head_slot, b * L:(b + 1) * L],
                             maxima_dram[slot % 2].rearrange("(p q) c -> p (q c)", p=3)).then_inc(mrow_loaded[slot % 2], 16)

            maxima_of(0, 0, use_of_maxima(0))

            def pair2(i, first=False, last=False):
                for ul in range(4):
                    u = 4 * i + ul
                    if not (last and ul == 3):
                        use = LAST_MAXIMA if last and ul == 2 else use_of_maxima(u + 1)
                        maxima_of(u + 1, (ul + 1) % 4, use)
                    if ul % 2 == 0:
                        hb = 2 * i + ul // 2 + 1
                        slot = (ul // 2 + 1) % 2
                        if not (first and ul == 0):
                            sp.wait_ge(sb_done[1], 2 * QB * u)
                            if not (last and ul == 2):
                                rows_of(1, hb, slot, qb_rows, kb_rows, qkb_loaded)
                        if not last:
                            sp.wait_ge(sa_done[1], use_of_block(u + AU - 1, QB - 1) + 1)
                            rows_of(1, hb + 1, 1 - slot, q_rows, k_rows, qk_loaded[1])
                    if not (first and ul == 0):
                        store_unit(1, u - 1, (ul - 1) % 2)

            pair2(0, first=True)
            with sp.Fori(1, PAIRS - 1) as i:
                pair2(i)
            pair2(PAIRS - 1, last=True)
            store_unit(1, U - 1, (U - 1) % 2)
            load_heads(1)

            out_tiles = out.rearrange("b (t p) d -> p (b t) d", p=P)
            for g in range(G):
                sp.wait_ge(out_ready, g + 1)
                sp.dma_start(out_tiles[:, g * TG:(g + 1) * TG, :], norm[:, g * TG:(g + 1) * TG, :]).then_inc(out_stored, 16)
            sp.wait_ge(out_stored, 16 * G)

        @block.gpsimd
        def _(pool):
            steps = [0]

            def chain(ins):
                steps[0] += 1
                ins.then_inc(pool_step, 1)
                pool.wait_ge(pool_step, steps[0])

            nc.gpsimd.iota(rel_pos, [[-1, 2 * L]], base=L - 1, channel_multiplier=0,
                           allow_small_or_imprecise_dtypes=True).then_inc(consts_ready, 1)
            chain(nc.gpsimd.memset(amp_sel[:], 1.0))
            chain(nc.gpsimd.affine_select(out=amp_sel[:], in_=amp_sel[:], compare_op=ALU.is_ge, fill=0.0, base=0,
                                          pattern=[[P, 2], [-NK, H]], channel_multiplier=1))
            chain(nc.gpsimd.affine_select(out=amp_sel[:], in_=amp_sel[:], compare_op=ALU.is_ge, fill=0.0,
                                          base=NK - 1, pattern=[[-P, 2], [NK, H]], channel_multiplier=-1))
            nc.gpsimd.memset(eps_col[:], EPS).then_inc(consts_ready, 1)
            chain(nc.gpsimd.memset(ident[:], 0.0))
            chain(nc.gpsimd.affine_select(out=ident[:], in_=ident[:], compare_op=ALU.not_equal, fill=1.0, base=0,
                                          pattern=[[-1, P]], channel_multiplier=1))
            chain(nc.gpsimd.tensor_copy(ident_b[:], ident[:]))
            chain(nc.gpsimd.memset(head_sel[:], 1.0))
            chain(nc.gpsimd.affine_select(out=head_sel[:], in_=head_sel[:], compare_op=ALU.is_ge, fill=0.0, base=0,
                                          pattern=[[1, D]], channel_multiplier=-DH))
            chain(nc.gpsimd.affine_select(out=head_sel[:], in_=head_sel[:], compare_op=ALU.is_ge, fill=0.0,
                                          base=DH - 1, pattern=[[-1, D]], channel_multiplier=DH))
            nc.gpsimd.iota(order[:], [[-1, E]], base=E, channel_multiplier=0,
                           allow_small_or_imprecise_dtypes=True).then_inc(consts_ready, 1)
            pool.wait_ge(consts_ready, 3)
            for rows in (q_rows, k_rows):
                chain(nc.gpsimd.memset(rows[32:64], 0.0))
                chain(nc.gpsimd.memset(rows[64:P], 0.0))
            chain(nc.gpsimd.memset(v_ring[:], 0.0))
            chain(nc.gpsimd.memset(v_ring[:, :, :, DH:DH + 1], 1.0))
            pool.sem_inc(ones_ready, 1)

            def v_of(a, h, slot, wait):
                if wait:
                    pool.wait_ge(av_done[a], B * (h - 1))
                pool.sem_inc(past_wait_pool, 1)
                nc.gpsimd.tensor_copy(v_ring[:, slot, :, 0:DH],
                                      v_nat[:, :, bass.ds(h * DH, DH)]).then_inc(v_ready[a], 1)

            pool.wait_ge(v_evac[0], G)
            def pair1(i, first=False):
                for l in range(4 * QB):
                    if l % (2 * QB) == 0:
                        v_of(0, 2 * i + l // (2 * QB), l // (2 * QB), not first)
                    if SHIFT_BY[l % QB] == "P":
                        pool.wait_ge(max_done[0], 4 * QB * i + l + 1)
                        t = logit[:, l % NT, :]
                        nc.gpsimd.tensor_tensor(t, t, bcast(row_max[:, l % QB:l % QB + 1], L),
                                                ALU.subtract).then_inc(shift_pool, 1)

            pair1(0, first=True)
            with pool.Fori(1, PAIRS) as i:
                pair1(i)

            pool.wait_ge(max_done[0], QB * U)
            pool.wait_ge(shift_pool, 4 * SHIFT_BY.count("P") * PAIRS)
            pool.wait_ge(v_ready[0], H)
            nc.gpsimd.memset(kb_rows[32:64], -1.0).then_inc(kb_minus, 1)
            pool.wait_ge(kb_minus, 1)
            nc.gpsimd.memset(kb_rows[64:P], 0.0).then_inc(kb_minus, 1)
            nc.gpsimd.memset(qb_rows[64:P], 0.0).then_inc(kb_minus, 1)
            pool.wait_ge(kb_minus, 3)
            nc.gpsimd.memset(qb_rows[32:64], 0.0).then_inc(kb_minus, 1)
            pool.wait_ge(kb_minus, 4)

            def split_maxima(u, slot):
                pool.wait_ge(max_done[1], use_of_block(u, QB - 1) + 1 if not isinstance(u, int) or u else QB)
                m, r = unit_max[:, slot, :], max_rest[:, slot]
                hi, mid, lo = (max_parts[:, slot, n * QB:(n + 1) * QB] for n in range(3))
                pool.sem_inc(past_wait_pool, 1)
                nc.gpsimd.tensor_copy(hi, m).then_inc(split_step, 1)
                pool.wait_ge(split_step, 4 * u + 1)
                nc.gpsimd.tensor_tensor(r[:, 0, :], m, hi, ALU.subtract).then_inc(split_step, 1)
                pool.wait_ge(split_step, 4 * u + 2)
                pool.sem_inc(past_wait_pool, 1)
                nc.gpsimd.tensor_copy(mid, r[:, 0, :]).then_inc(split_step, 1)
                pool.wait_ge(split_step, 4 * u + 3)
                nc.gpsimd.tensor_tensor(lo, r[:, 0, :], mid, ALU.subtract).then_inc(split_step, 1)

            pool.wait_ge(v_evac[1], G)
            pool.wait_ge(av_done[0], U)
            split_maxima(0, 0)
            split_maxima(1, 1)

            def pair2(i, first=False, last=False):
                for ul in range(4):
                    if ul % 2 == 0:
                        v_of(1, 2 * i + ul // 2, ul // 2, not first)
                    if not (last and ul >= 2):
                        split_maxima(4 * i + ul + AU, ul % 2)

            pair2(0, first=True)
            with pool.Fori(1, PAIRS - 1) as i:
                pair2(i)
            pair2(PAIRS - 1, last=True)

        @block.scalar
        def _(act):
            act.wait_ge(consts_ready, 1)
            act.wait_ge(bias_loaded, 48)
            for t in range(2):
                nc.scalar.activation(bias_e[:, t, :], rel_pos, ACT.Square, bias=bias_par[:, 0, t:t + 1]).then_inc(bias_sq, 1)
            act.wait_ge(sharp_ready, 2)
            for t in range(2):
                act.wait_ge(bias_sq, t + 1)
                nc.scalar.activation(bias_e[:, t, :], bias_e[:, t, :], ACT.Exp,
                                     scale=neg_sharp[:, t:t + 1]).then_inc(bias_exp, 1)
            act.wait_ge(w_t_mm, 1)
            nc.scalar.copy(w_in_t[:].rearrange("p c d -> p (c d)"), bank[:, 4, 0:3 * D]).then_inc(w_t_ready, 1)

            def norm_std(n):
                for g in range(G):
                    act.wait_ge(ln_aggr[n], TG * (g + 1))
                    ts = slice(g * TG, (g + 1) * TG)
                    nc.scalar.activation(std[:, ts], meanvar[:, ts, 1], ACT.Sqrt, bias=eps_col[:, 0:1]).then_inc(ln_std[n], 1)

            def feature_major(a, par):
                for g in range(G):
                    act.wait_ge(tp_done[a], g + 1)
                    dst, src = feat[:, g * N:(g + 1) * N], bank[:, g, :]
                    if par is None:
                        nc.scalar.copy(dst, src).then_inc(feat_ready[a], 1)
                    else:
                        nc.scalar.activation(dst, src, ACT.Identity, scale=ln_par[:, par:par + 1],
                                             bias=ln_par[:, par + 1:par + 2]).then_inc(feat_ready[a], 1)

            def projections(a):
                for g in range(G):
                    cols = slice(g * N, (g + 1) * N)
                    act.wait_ge(q_mm[a], g + 1)
                    nc.scalar.activation(parts[:, 0, 0, cols], bank[:, 4, :], ACT.Copy, scale=SCALE).then_inc(part_hi[a], 1)
                    act.wait_ge(k_mm[a], g + 1)
                    nc.scalar.copy(parts[:, 1, 0, cols], bank[:, 5, :]).then_inc(part_hi[a], 1)
                    act.wait_ge(v_mm[a], g + 1)
                    nc.scalar.copy(v_nat[:, g * TG:(g + 1) * TG, :],
                                   bank[:, 6, :].rearrange("p (t d) -> p t d", t=TG)).then_inc(v_evac[a], 1)
                    for s in range(2):
                        act.wait_ge(part_rest[a], 2 * g + s + 1)
                        nc.scalar.copy(parts[:, s, 1, cols], rest[:, s, :]).then_inc(part_mid[a], 1)

            def evacuate(a, u, slot, wait):
                act.wait_ge(av_done[a], u + 1)
                if wait:
                    act.wait_ge(o_stored[a][slot], 8 * (u - slot))
                nc.scalar.copy(o_ring[:, slot, :], AV[slot][:, 0:L // 4]).then_inc(o_ready[a], 1)

            norm_std(0)
            feature_major(0, None)
            projections(0)

            def shift(i, l):
                if SHIFT_BY[l % QB] == "A":
                    act.wait_ge(max_done[0], 4 * QB * i + l + 1)
                    t = logit[:, l % NT, :]
                    nc.scalar.activation(t, t, ACT.Identity, scale=-1.0,
                                         bias=row_max[:, l % QB:l % QB + 1]).then_inc(shift_act, 1)

            def pair1(i, first=False, last=False):
                for l in range(4 * QB):
                    ul, qb = l // QB, l % QB
                    if qb == 1 and not (first and ul < 2):
                        evacuate(0, 4 * i + ul - 2, ul % 2, not (first and ul < 4))
                    if qb == 0 and not (first and ul < 2):
                        act.wait_ge(av_done[0], 4 * i + ul - 1)
                    for j in range(2):
                        act.wait_ge(sb_done[0], 8 * QB * i + 2 * l + j + 1)
                        nc.scalar.activation(prob[:, ul % 2, 4 * j:4 * j + 4, qb * P:(qb + 1) * P],
                                             SB[j].rearrange("p (k q) -> p k q", k=4), ACT.Exp,
                                             scale=-1.0 if SHIFT_BY[qb] == "A" else 1.0).then_inc(exp_done[0], 1)
                    if not (last and l + 2 >= 4 * QB):
                        shift(i, l + 2)

            for l in range(2):
                shift(0, l)
            pair1(0, first=True)
            with act.Fori(1, PAIRS - 1) as i:
                pair1(i)
            pair1(PAIRS - 1, last=True)
            for u in (U - 2, U - 1):
                evacuate(0, u, u % 2, True)

            for g in range(G):
                act.wait_ge(nat_mm[0], g + 1)
                nc.scalar.copy(norm[:, g * TG:(g + 1) * TG, :],
                               bank[:, 4 + g, :].rearrange("p (t d) -> p t d", t=TG)).then_inc(nat_ready[0], 1)
            norm_std(1)
            norm_std(2)
            norm_std(3)
            feature_major(1, 0)
            projections(1)

            def pair2(i, first=False, last=False):
                for ul in range(4):
                    u = 4 * i + ul
                    if not (first and ul < 2):
                        act.wait_ge(av_done[1], u - 1)
                    for kb in range(QB):
                        if kb == 3 and not (first and ul < 1):
                            evacuate(1, u - 1, (ul - 1) % 2, not (first and ul < 3))
                        for half in range(2):
                            act.wait_ge(sb_done[1], 8 * QB * i + 2 * (QB * ul + kb) + half + 1)
                            nc.scalar.activation(prob[:, ul % 2, kb, half * N:(half + 1) * N], SB[half],
                                                 ACT.Exp).then_inc(exp_done[1], 1)

            pair2(0, first=True)
            with act.Fori(1, PAIRS) as i:
                pair2(i)
            evacuate(1, U - 1, (U - 1) % 2, True)

            norm_std(4)
            feature_major(2, 2)
            for q in range(E * G):
                for c in range(HC):
                    act.wait_ge(hid_mm, HC * q + c + 1)
                    if q >= 2 and c == 0:
                        act.wait_ge(moe_mm, q - 1)
                    nc.scalar.activation(hidden[:, q % 2, c, :], bank[:, c, :],
                                         ACT.Gelu_apprx_tanh).then_inc(hid_ready, 1)
            norm_std(5)

        @block.vector
        def _(dve):
            dve.wait_ge(bias_loaded, 48)
            nc.vector.tensor_scalar(neg_sharp[:], bias_par[:, 2, :], -1.0, None, ALU.mult).then_inc(sharp_ready, 1)
            dve.wait_ge(sharp_ready, 1)
            nc.vector.tensor_tensor(neg_sharp[:], neg_sharp[:], bias_par[:, 2, :], ALU.min).then_inc(sharp_ready, 1)

            def norm_stats(n, src, wait):
                for t in range(TT):
                    if t % TG == 0:
                        wait(t // TG)
                    nc.vector.bn_stats(stats[:, t, :], src[:, t, :]).then_inc(ln_stats[n], 1)
                for t in range(TT):
                    dve.wait_ge(ln_stats[n], t + 1)
                    nc.vector.bn_aggr(meanvar[:, t, :], stats[:, t, :]).then_inc(ln_aggr[n], 1)

            def norm_apply(n, src, dst, then=None):
                for g in range(G):
                    ts = slice(g * TG, (g + 1) * TG)
                    dve.wait_ge(ln_std[n], g + 1)
                    nc.vector.reciprocal(rstd[:, ts], std[:, ts]).then_inc(ln_rstd[n], 1)
                    dve.wait_ge(ln_rstd[n], g + 1)
                    for t in range(g * TG, (g + 1) * TG):
                        nc.vector.tensor_scalar(dst[:, t, :], src[:, t, :], meanvar[:, t, 0:1], rstd[:, t:t + 1],
                                                ALU.subtract, ALU.mult).then_inc(ln_out[n], 1)
                    if then:
                        dve.wait_ge(ln_out[n], TG * (g + 1))
                        then(g, ts)

            norm_stats(0, x_res, lambda g: dve.wait_ge(x_loaded[g], 16))
            norm_apply(0, x_res, norm)
            dve.wait_ge(ones_ready, 1)
            for t in range(2):
                ins = nc.vector.tensor_scalar(amp_sel[:, t, :], amp_sel[:, t, :], bias_par[:, 1, t:t + 1], None, ALU.mult)
            ins.then_inc(amp_ready, 1)
            for c in range(4):
                dve.wait_ge(bias_mm, c + 1)
                nc.vector.tensor_copy(bias_row[:, c * N:(c + 1) * N], bank[0:H, c, :]).then_inc(bias_out, 1)

            def projections(a):
                for g in range(G):
                    cols = slice(g * N, (g + 1) * N)
                    for s in range(2):
                        dve.wait_ge(part_hi[a], 2 * g + s + 1)
                        if g:
                            dve.wait_ge(part_lo[a], 2 * (g - 1) + s + 1)
                        nc.vector.scalar_tensor_tensor(rest[:, s, :], bank[:, 4 + s, :], SCALE if s == 0 else 1.0,
                                                       parts[:, s, 0, cols], ALU.mult, ALU.subtract).then_inc(part_rest[a], 1)
                    for s in range(2):
                        dve.wait_ge(part_mid[a], 2 * g + s + 1)
                        nc.vector.tensor_tensor(parts[:, s, 2, cols], rest[:, s, :], parts[:, s, 1, cols],
                                                ALU.subtract).then_inc(part_lo[a], 1)

            projections(0)

            def shift(i, l):
                if SHIFT_BY[l % QB] == "D":
                    dve.wait_ge(max_done[0], 4 * QB * i + l + 1)
                    t = logit[:, l % NT, :]
                    nc.vector.tensor_scalar(t, t, row_max[:, l % QB:l % QB + 1], None, ALU.subtract).then_inc(shift_dve, 1)

            def pair1(i, first=False):
                for l in range(4 * QB):
                    s, qb = 4 * QB * i + l, l % QB
                    head_slot = l // (2 * QB)
                    if l % (2 * QB) == 0:
                        dve.wait_ge(tab_loaded[head_slot], 16 * (i + 1))
                    dve.wait_ge(sa_done[0], s + 1)
                    if not (first and l < NT):
                        dve.wait_ge(sb_done[0], 2 * (s - NT) + 2)
                    dve.sem_inc(past_wait_dve, 1)
                    tab = bias_tab[:, head_slot, qb * P + L - 1:qb * P + L]
                    bias = bass.AP(tab.tensor, tab.offset, [list(tab.ap[0]), [-1, L]])
                    nc.vector.tensor_tensor_reduce(
                        out=logit[:, l % NT, :], in0=SA[l % 2].rearrange("p a n -> p (a n)"), in1=bias,
                        scale=1.0, scalar=LEAST, op0=ALU.add, op1=ALU.max,
                        accum_out=row_max[:, qb:qb + 1]).then_inc(max_done[0], 1)
                    if l:
                        shift(i, l - 1)
                    if l == 4 * QB - 1:
                        shift(i, l)
                pass

            pair1(0, first=True)
            with dve.Fori(1, PAIRS) as i:
                pair1(i)

            def scale_heads(a):
                dve.wait_ge(sums_loaded[a], 16 * B)
                for g in range(G):
                    cols = slice(g * N, (g + 1) * N)
                    nc.vector.reciprocal(sums[:, cols], sums[:, cols]).then_inc(recip_done[a], 1)
                for g in range(G):
                    cols = slice(g * N, (g + 1) * N)
                    dve.wait_ge(heads_loaded[a][g], 32)
                    dve.wait_ge(spread_mm[a], g + 1)
                    nc.vector.tensor_tensor(feat[:, cols], feat[:, cols], bank[:, g, :], ALU.mult).then_inc(heads_scaled[a], 1)

            scale_heads(0)
            norm_stats(1, norm, lambda g: dve.wait_ge(nat_ready[0], g + 1))

            def add_x(g, ts):
                nc.vector.tensor_tensor(x_res[:, ts, :], x_res[:, ts, :], norm[:, ts, :], ALU.add).then_inc(x_added, 1)

            norm_apply(1, norm, norm, add_x)
            norm_stats(2, x_res, lambda g: dve.wait_ge(x_added, g + 1))
            norm_apply(2, x_res, y_res)
            norm_stats(3, y_res, lambda g: dve.wait_ge(ln_out[2], TG * (g + 1)))
            norm_apply(3, y_res, norm)
            projections(1)

            def block_max(u, qb, use, slot):
                dve.wait_ge(sa_done[1], use + 1)
                nc.vector.tensor_reduce(unit_max[:, slot, qb:qb + 1], SA[use_parity[0]].rearrange("p a n -> p (a n)"),
                                        AX.X, ALU.max).then_inc(max_done[1], 1)

            use_parity = [0]

            def maxima_out(use, parity, slot, stored):
                dve.wait_ge(sa_done[1], use + 1)
                if stored is not None:
                    dve.wait_ge(mrow_stored, 16 * stored)
                nc.vector.tensor_copy(max_rows[:, slot, :],
                                      SA[parity][0:3 * QB, 0, 0:P // 2].bitcast(bf16)).then_inc(max_done[1], 1)

            for qb in range(QB):
                use_parity[0] = qb % 2
                block_max(0, qb, qb, 0)
            for qb in range(QB):
                use_parity[0] = use_of_block(1, qb) % 2
                block_max(1, qb, use_of_block(1, qb), 1)
                if qb == 2:
                    maxima_out(use_of_maxima(0), use_of_maxima(0) % 2, 0, None)

            def pair2(i, first=False, last=False):
                for ul in range(4):
                    u, lu = 4 * i + ul, ul + AU
                    done = last and ul >= 2
                    for qb in range(QB):
                        if not done:
                            use_parity[0] = use_of_block(lu, qb) % 2
                            block_max(u + AU, qb, use_of_block(u + AU, qb), ul % 2)
                        if qb == 2 and not (last and ul == 3):
                            use = LAST_MAXIMA if done else use_of_maxima(u + 1)
                            parity = (LAST_MAXIMA if done else use_of_maxima(lu - 1)) % 2
                            maxima_out(use, parity, (ul + 1) % 2, None if first and ul == 0 else u)

            pair2(0, first=True)
            with dve.Fori(1, PAIRS - 1) as i:
                pair2(i)
            pair2(PAIRS - 1, last=True)

            scale_heads(1)
            for g in range(G):
                ts = slice(g * TG, (g + 1) * TG)
                dve.wait_ge(nat_mm[1], g + 1)
                nc.vector.tensor_tensor(y_res[:, ts, :], y_res[:, ts, :],
                                        bank[:, 4 + g, :].rearrange("p (t d) -> p t d", t=TG), ALU.add).then_inc(nat_ready[1], 1)
            norm_stats(4, y_res, lambda g: dve.wait_ge(nat_ready[1], g + 1))
            norm_apply(4, y_res, norm)

            n = [0]

            def chain(ins):
                n[0] += 1
                ins.then_inc(gate_step, 1)
                dve.wait_ge(gate_step, n[0])

            dve.wait_ge(gate_mm, 1)
            dve.wait_ge(weights_loaded, 16 * 9)
            gb = gate_b_sb[:, :]
            gate_b_all = bass.AP(gb.tensor, gb.offset, [list(gb.ap[0]), [0, TT], [1, E]])
            od = order[:, :]
            order_all = bass.AP(od.tensor, od.offset, [list(od.ap[0]), [0, TT], [1, E]])
            gm = gate_max[:, :, :]
            max_all = bass.AP(gm.tensor, gm.offset, [list(gm.ap[0]), [1, TT], [0, E]])
            chain(nc.vector.tensor_tensor(gate[:], bank[:, 7, 0:TT * E].rearrange("p (t e) -> p t e", t=TT), gate_b_all, ALU.add))
            chain(nc.vector.tensor_reduce(gate_max[:], gate[:], AX.X, ALU.max))
            chain(nc.vector.tensor_tensor(onehot[:], gate[:], max_all, ALU.is_equal))
            chain(nc.vector.tensor_tensor(gate[:], onehot[:], order_all, ALU.mult))
            chain(nc.vector.tensor_reduce(gate_max[:], gate[:], AX.X, ALU.max))
            chain(nc.vector.tensor_tensor(onehot[:], gate[:], max_all, ALU.is_equal))
            for q in range(E * G):
                e, g = divmod(q, G)
                dve.wait_ge(moe_mm, q + 1)
                for tt in range(TG):
                    t = g * TG + tt
                    if tt == 0 and e:
                        dve.wait_ge(moe_added, TG * (q - G + 1))
                    nc.vector.scalar_tensor_tensor(y_res[:, t, :], bank[:, 4 + q % 2, tt * P:(tt + 1) * P],
                                                   onehot[:, t, e:e + 1], y_res[:, t, :], ALU.mult, ALU.add).then_inc(moe_added, 1)

            norm_stats(5, y_res, lambda g: dve.wait_ge(moe_added, TG * (G * (E - 1) + g + 1)))

            def add_out(g, ts):
                nc.vector.tensor_tensor(norm[:, ts, :], x_res[:, ts, :], norm[:, ts, :], ALU.add).then_inc(out_ready, 1)

            norm_apply(5, y_res, norm, add_out)

        @block.tensor
        def _(pe):
            pe.wait_ge(ones_ready, 1)
            pe.wait_ge(weights_loaded, 16 * 9)
            for c in range(3):
                ins = nc.tensor.transpose(bank[:, 4, c * D:(c + 1) * D], w_in_nat[:, c, :], ident[:])
            ins.then_inc(w_t_mm, 1)
            pe.wait_ge(amp_ready, 1)
            pe.wait_ge(bias_exp, 2)
            for c in range(4):
                for t in range(2):
                    ins = nc.tensor.matmul(bank[0:H, c, :], amp_sel[:, t, :], bias_e[:, t, c * N:(c + 1) * N],
                                           start=(t == 0), stop=(t == 1))
                ins.then_inc(bias_mm, 1)

            def transposes(a, ln):
                for g in range(G):
                    pe.wait_ge(ln_out[ln], TG * (g + 1))
                    for tt in range(TG):
                        ins = nc.tensor.transpose(bank[:, g, tt * P:(tt + 1) * P], norm[:, g * TG + tt, :], ident[:])
                    ins.then_inc(tp_done[a], 1)

            def projections(a, wq, wk, wv):
                for g in range(G):
                    cols = slice(g * N, (g + 1) * N)
                    pe.wait_ge(feat_ready[a], g + 1)
                    if g:
                        pe.wait_ge(part_rest[a], 2 * g - 1)
                    nc.tensor.matmul(bank[:, 4, :], wq, feat[:, cols], start=True, stop=True).then_inc(q_mm[a], 1)
                    if g:
                        pe.wait_ge(part_rest[a], 2 * g)
                    nc.tensor.matmul(bank[:, 5, :], wk, feat[:, cols], start=True, stop=True).then_inc(k_mm[a], 1)
                    if g:
                        pe.wait_ge(v_evac[a], g)
                    for tt in range(TG):
                        t = g * TG + tt
                        ins = nc.tensor.matmul(bank[:, 6, tt * P:(tt + 1) * P], feat[:, t * P:(t + 1) * P], wv,
                                               start=True, stop=True)
                    ins.then_inc(v_mm[a], 1)

            pe.wait_ge(bias_out, 4)
            pe.wait_ge(w_t_ready, 1)
            transposes(0, 0)
            projections(0, w_in_t[:, 2, :], w_in_t[:, 0, :], w_in_t[:, 1, :])

            def scores_a(slot, head_slot, b, qb, sem_done):
                lhs = q_rows[:, head_slot, b * L + qb * P:b * L + (qb + 1) * P]
                for j in range(2):
                    ins = nc.tensor.matmul(SA[slot][:, j, :], lhs,
                                           k_rows[:, head_slot, b * L + j * N:b * L + (j + 1) * N], start=True, stop=True)
                ins.then_inc(sem_done, 1)

            def weigh_v(a, ul, kb, last_inc):
                head_slot, b = (ul // B) % 2, ul % B
                W = L // 4
                for c in range(4):
                    ins = nc.tensor.matmul(AV[ul % 2][VM * c:VM * (c + 1), 0:W], v_ring[:, head_slot, b * QB + kb, :],
                                           prob[:, ul % 2, kb, c * W:(c + 1) * W], start=(kb == 0), stop=(kb == QB - 1),
                                           tile_position=(0, VM * c))
                if last_inc:
                    ins.then_inc(av_done[a], 1)

            def before_av(a, i, ul, guard_bank):
                u = 4 * i + ul
                if ul % 2 == 0:
                    pe.wait_ge(v_ready[a], 2 * i + ul // 2 + 1)
                if guard_bank:
                    pe.wait_ge(o_ready[a], u - 1)

            pe.wait_ge(part_rest[0], 2 * G)
            pe.wait_ge(v_evac[0], G)

            def block_a(i, l, first):
                s = 4 * QB * i + l
                ul, qb = l // QB, l % QB
                if l % (2 * QB) == 0:
                    pe.wait_ge(qk_loaded[0][(ul // B) % 2], 16 * QK_DMAS * (i + 1 + l // (4 * QB)))
                if not (first and l < 2):
                    pe.wait_ge(max_done[0], s - 1)
                scores_a(l % 2, (ul // B) % 2, ul % B, qb, sa_done[0])

            def pair1(i, first=False, last=False):
                for l in range(4 * QB):
                    ul, qb = l // QB, l % QB
                    pe.wait_ge(shift_sem[SHIFT_BY[qb]], shift_count(i, l))
                    for j in range(2):
                        if not (first and l == 0):
                            pe.wait_ge(exp_done[0], 8 * QB * i + 2 * l + j - 1)
                        for k in range(4):
                            ins = nc.tensor.transpose(SB[j][:, k * P:(k + 1) * P],
                                                      logit[:, l % NT, (4 * j + k) * P:(4 * j + k + 1) * P], ident[:])
                        ins.then_inc(sb_done[0], 1)
                    if not (last and l + 3 >= 4 * QB):
                        block_a(i, l + 3, first)
                    if not (first and ul == 0):
                        if qb == 0:
                            before_av(0, i, ul - 1, not (first and ul < 3))
                            pe.wait_ge(exp_done[0], 2 * QB * (4 * i + ul))
                        weigh_v(0, (ul - 1) % 4, qb, qb == QB - 1)

            for l in range(3):
                block_a(0, l, True)
            pair1(0, first=True)
            with pe.Fori(1, PAIRS - 1) as i:
                pair1(i)
            pair1(PAIRS - 1, last=True)
            before_av(0, PAIRS - 1, 3, True)
            pe.wait_ge(exp_done[0], 2 * QB * U)
            for kb in range(QB):
                weigh_v(0, 3, kb, kb == QB - 1)

            def spread(a):
                for g in range(G):
                    pe.wait_ge(recip_done[a], g + 1)
                    nc.tensor.matmul(bank[:, g, :], head_sel[:], sums[:, g * N:(g + 1) * N], start=True, stop=True).then_inc(spread_mm[a], 1)

            spread(0)
            pe.wait_ge(o_ready[0], U)
            for g in range(G):
                pe.wait_ge(heads_scaled[0], g + 1)
                for tt in range(TG):
                    t = g * TG + tt
                    ins = nc.tensor.transpose(bank[:, 4 + g, tt * P:(tt + 1) * P], feat[:, t * P:(t + 1) * P], ident[:])
                ins.then_inc(nat_mm[0], 1)
            pe.wait_ge(nat_ready[0], G)
            transposes(1, 3)
            projections(1, w_qkv_sb[:, 0, :], w_qkv_sb[:, 1, :], w_qkv_sb[:, 2, :])

            pe.wait_ge(feat_ready[1], G)
            pe.wait_ge(part_rest[1], 2 * G)
            pe.wait_ge(v_evac[1], G)

            def block_a2(lu, qb, use, guard, loads=None):
                if loads is not None:
                    pe.wait_ge(qk_loaded[1][(lu // B) % 2], 16 * QK_DMAS * loads)
                if guard:
                    pe.wait_ge(max_done[1], use - 1)
                parity = (qb if lu == 0 else use_of_block(lu, qb)) % 2
                scores_a(parity, (lu // B) % 2, lu % B, qb, sa_done[1])

            def maxima_t(u, use, parity, slot):
                pe.wait_ge(split_step, 4 * u + 4)
                pe.wait_ge(max_done[1], use - 1)
                nc.tensor.transpose(SA[parity][0:3 * QB, 0, 0:P // 2].bitcast(bf16), max_parts[:, slot, :],
                                    ident_b[:]).then_inc(sa_done[1], 1)

            for qb in range(QB):
                block_a2(0, qb, qb, qb >= 2, 1 if qb == 0 else None)
            for qb in range(QB):
                block_a2(1, qb, use_of_block(1, qb), True)
                if qb == 2:
                    maxima_t(0, use_of_maxima(0), use_of_maxima(0) % 2, 0)

            def pair2(i, first=False, last=False):
                for ul in range(4):
                    u, lu = 4 * i + ul, ul + AU
                    head_slot, b = ul // B, ul % B
                    done = last and ul >= 2
                    if b == 0:
                        pe.wait_ge(qkb_loaded[head_slot], 16 * QK_DMAS * (i + 1))
                    pe.wait_ge(mrow_loaded[ul % 2], 16 * (2 * i + ul // 2 + 1))
                    for kb in range(QB):
                        lhs = kb_rows[:, head_slot, b * L + kb * P:b * L + (kb + 1) * P]
                        for half in range(2):
                            if not (first and ul == 0 and kb == 0):
                                pe.wait_ge(exp_done[1], 8 * QB * i + 2 * (QB * ul + kb) + half - 1)
                            nc.tensor.matmul(SB[half], lhs, qb_rows[:, head_slot, b * L + half * N:b * L + (half + 1) * N],
                                             start=True, stop=True).then_inc(sb_done[1], 1)
                        if not done:
                            block_a2(lu, kb, use_of_block(u + AU, kb), True,
                                     i + 1 + lu // 4 if kb == 0 and lu % 2 == 0 else None)
                        if kb == 2 and not (last and ul == 3):
                            maxima_t(u + 1, LAST_MAXIMA if done else use_of_maxima(u + 1),
                                     (LAST_MAXIMA if done else use_of_maxima(lu - 1)) % 2, (ul + 1) % 2)
                        if kb < 2:
                            if not (first and ul == 0):
                                pe.wait_ge(exp_done[1], 2 * (8 * (4 * i + ul - 1) + kb + 6) + 2)
                                weigh_v(1, (ul - 1) % 4, kb + 6, kb == 1)
                        else:
                            if kb == 2:
                                before_av(1, i, ul, not (first and ul < 2))
                            pe.wait_ge(exp_done[1], 2 * (8 * (4 * i + ul) + kb - 2) + 2)
                            weigh_v(1, ul, kb - 2, False)

            pair2(0, first=True)
            with pe.Fori(1, PAIRS - 1) as i:
                pair2(i)
            pair2(PAIRS - 1, last=True)
            pe.wait_ge(exp_done[1], 2 * QB * U)
            for kb in (6, 7):
                weigh_v(1, 3, kb, kb == 7)

            spread(1)
            pe.wait_ge(o_ready[1], U)
            for g in range(G):
                pe.wait_ge(heads_scaled[1], g + 1)
                for tt in range(TG):
                    t = g * TG + tt
                    ins = nc.tensor.matmul(bank[:, 4 + g, tt * P:(tt + 1) * P], feat[:, t * P:(t + 1) * P], w_proj_sb[:],
                                           start=True, stop=True)
                ins.then_inc(nat_mm[1], 1)

            pe.wait_ge(nat_ready[1], G)
            transposes(2, 4)
            for t in range(TT):
                pe.wait_ge(feat_ready[2], t // TG + 1)
                ins = nc.tensor.matmul(bank[:, 7, t * E:(t + 1) * E], feat[:, t * P:(t + 1) * P], gate_w_sb[:], start=True, stop=True)
            ins.then_inc(gate_mm, 1)
            pe.wait_ge(moe_loaded, 32)

            def up(q):
                e, g = divmod(q, G)
                for c in range(HC):
                    if q:
                        pe.wait_ge(hid_ready, HC * (q - 1) + c + 1)
                    nc.tensor.matmul(bank[:, c, :], w1_sb[:, e, c * P:(c + 1) * P], feat[:, g * N:(g + 1) * N],
                                     start=True, stop=True).then_inc(hid_mm, 1)

            def down(q):
                e, g = divmod(q, G)
                pe.wait_ge(hid_ready, HC * (q + 1))
                if q >= 2:
                    pe.wait_ge(moe_added, TG * (q - 1))
                for tt in range(TG):
                    for c in range(HC):
                        ins = nc.tensor.matmul(bank[:, 4 + q % 2, tt * P:(tt + 1) * P], hidden[:, q % 2, c, tt * P:(tt + 1) * P],
                                               w2_sb[:, e, c, :], start=(c == 0), stop=(c == HC - 1))
                ins.then_inc(moe_mm, 1)

            up(0)
            for q in range(1, E * G):
                up(q)
                down(q - 1)
            down(E * G - 1)


_INS = ['L0_attn_x', 'L0_attn_w_in', 'L0_attn_kernel_offsets', 'L0_attn_kernel_amplitudes', 'L0_attn_kernel_sharpness',
        'L0_ffn_ln1_w', 'L0_ffn_ln1_b', 'L0_ffn_w_qkv', 'L0_ffn_w_proj', 'L0_ffn_ln2_w', 'L0_ffn_ln2_b',
        'L0_ffn_gate_w', 'L0_ffn_gate_b', 'L0_ffn_w1', 'L0_ffn_w2']


def kernel(**inputs):
    import numpy as _np
    import concourse.bacc as _bacc
    from concourse import mybir as _mybir
    from concourse.bass_utils import run_bass_kernel_spmd as _run

    nc = _bacc.Bacc("TRN2", target_bir_lowering=False, num_devices=1)
    arrays, args = {}, []
    for name in _INS:
        a = _np.ascontiguousarray(inputs[name])
        arrays[f"in_{name}_dram"] = a
        args.append(nc.dram_tensor(f"in_{name}_dram", a.shape, _mybir.dt.from_np(a.dtype), kind="ExternalInput").ap())
    shape = inputs['L0_attn_x'].shape
    args.append(nc.dram_tensor("out_dram", shape, _mybir.dt.float32, kind="ExternalOutput").ap())
    sandwich_kernel(nc, *args)
    r = _run(nc, [arrays], core_ids=[0])
    return r.results[0]["out_dram"]
```

```python
import concourse.bass as bass
from concourse import mybir
from contextlib import ExitStack
import numpy as np


def sandwich_kernel(nc, x, w_in, offsets, amplitudes, sharpness, ln1_w, ln1_b, w_qkv, w_proj,
                    ln2_w, ln2_b, gate_w, gate_b, w1, w2, out):
    fp32, bf16 = mybir.dt.float32, mybir.dt.bfloat16
    ALU, ACT, AX = mybir.AluOpType, mybir.ActivationFunctionType, mybir.AxisListType

    B, L, D = x.shape
    P = 128
    T = B * L
    TT = T // P
    H = offsets.shape[0]
    NK = offsets.shape[1]
    DH = D // H
    SCALE = float(np.float32(1.0) / np.sqrt(np.float32(DH)))
    EPS = 1e-5
    E, _, HID = w1.shape
    HC = HID // P
    U = B * H
    QB = L // P
    N = 512
    G = T // N
    TG = N // P
    LEAST = -3.0e38
    PAIRS = H // 2
    RUNS = [(0, 3, 0), (3, 2, 1), (5, 1, 2)]
    KR = 6 * DH
    QK_DMAS = 2 * len(RUNS)
    REL = 2 * L - 1
    TAW = 2 * L - P
    VM = 32

    NS = -(-((T - E) // P + E) // 4) * 4
    RW = D + 1
    slots_dram = nc.dram_tensor("slots", (NS * P, RW), fp32, kind="Internal").ap()
    moe_dram = nc.dram_tensor("moe_out", (T + NS * P, D), fp32, kind="Internal").ap()
    parts_dram = [nc.dram_tensor(f"parts{a}", (2, 3, D, T), bf16, kind="Internal").ap() for a in range(2)]
    heads_dram = [nc.dram_tensor(f"heads{a}", (U, P, L // 4), fp32, kind="Internal").ap() for a in range(2)]
    maxima_dram = nc.dram_tensor("maxima_rows", (2, 3 * QB, P), bf16, kind="Internal").ap()
    bias_dram = nc.dram_tensor("bias_rows", (H, 2 * L), fp32, kind="Internal").ap()

    with ExitStack() as ctx:
        def sb(name, shape, dt=fp32):
            return ctx.enter_context(nc.sbuf_tensor(name, shape, dt))

        def sem(name):
            return ctx.enter_context(nc.semaphore(name))

        x_res = sb("x_res", [P, TT, D])
        y_res = sb("y_res", [P, TT, D])
        norm = sb("norm", [P, TT, D])
        feat = sb("feat", [P, T])
        v_nat = sb("v_nat", [P, TT, D])
        sums = v_nat[0:H].rearrange("p t d -> p (t d)")
        q_rows = sb("q_rows", [P, 2, T], bf16)
        k_rows = sb("k_rows", [P, 2, T], bf16)
        tables = sb("tables", [P, 4096])
        bias_tab = tables[:, 0:2 * TAW].rearrange("p (s c) -> p s c", s=2)
        qb_rows = tables[:, 0:T].bitcast(bf16).rearrange("p (s n) -> p s n", s=2)
        kb_rows = tables[:, T:2 * T].bitcast(bf16).rearrange("p (s n) -> p s n", s=2)
        NT = 4
        logit = sb("logit", [P, NT, L])
        prob_mem = sb("prob_mem", [P, 2 * QB * L])
        prob = prob_mem[:, :].rearrange("p (s k q) -> p s k q", s=2, k=QB)
        bias_e = prob_mem[:, 0:4096].rearrange("p (t n) -> p t n", t=2)
        rel_pos = prob_mem[:, 4096:6144]
        bias_row = prob_mem[0:H, 6144:8192]
        parts = prob_mem[:, 8192:14336].bitcast(bf16).rearrange("p (s t n) -> p s t n", s=2, t=3)
        rest = prob_mem[:, 14336:15360].rearrange("p (s n) -> p s n", s=2)
        WE = 2 * HID
        at = [0]

        def inside(n):
            at[0] += n
            return prob_mem[:, at[0] - n:at[0]]

        token_rows = inside(TT * RW).rearrange("p (t c) -> p t c", t=TT)
        slot_rows = inside(NS * RW).rearrange("p (j c) -> p j c", j=NS)
        slot_feat = inside(NS * P)
        hidden = inside(2 * HID).rearrange("p (r c n) -> p r c n", r=2, c=HC)
        w_ring = inside(4 * WE).rearrange("p (r w) -> p r w", r=4)
        y_ring = inside(4 * D).rearrange("p (r d) -> p r d", r=4)
        assert at[0] <= 2 * QB * L
        v_ring = sb("v_ring", [P, 2, TT, VM])
        o_ring = sb("o_ring", [P, 2, L // 4])
        w_in_nat = sb("w_in_nat", [P, 3, D])
        w_in_t = sb("w_in_t", [P, 3, D])
        w_qkv_sb = sb("w_qkv_sb", [P, 3, D])
        w_proj_sb = sb("w_proj_sb", [P, D])
        gate_w_sb = sb("gate_w_sb", [P, E])
        gate_b_sb = sb("gate_b_sb", [P, E])
        w_moe = sb("w_moe", [P, E, 2 * HID])
        ln_par = sb("ln_par", [P, 4])
        bias_par = sb("bias_par", [P, 3, 2])
        neg_sharp = sb("neg_sharp", [P, 2])
        amp_sel = sb("amp_sel", [P, 2, H])
        ident = sb("ident", [P, P])
        ident_b = sb("ident_b", [P, P], bf16)
        head_sel = sb("head_sel", [H, D])
        eps_col = sb("eps_col", [P, 1])
        order = sb("order", [P, E])
        stats = sb("stats", [P, TT, 6])
        meanvar = sb("meanvar", [P, TT, 2])
        std = sb("std", [P, TT])
        rstd = sb("rstd", [P, TT])
        row_max = sb("row_max", [P, QB])
        unit_max = sb("unit_max", [P, 2, QB])
        max_rest = sb("max_rest", [P, 2, 2, QB])
        max_parts = sb("max_parts", [P, 2, 3 * QB], bf16)
        max_rows = sb("max_rows", [3 * QB, 2, P], bf16)
        gate = sb("gate", [P, TT, E])
        gate_max = sb("gate_max", [P, TT, 1])
        onehot = sb("onehot", [P, TT + 1, E], bf16)
        before = sb("before", [P, P], bf16)
        ones_b = sb("ones_b", [P, P], bf16)
        zeros = sb("zeros", [P, D])
        lower = sb("lower", [P, E, E])
        steps_of_tile = sb("steps_of_tile", [P, TT])
        tile_no = sb("tile_no", [P, NS])
        token_no = sb("token_no", [P, TT])
        spare_no = sb("spare_no", [P, NS])
        counts = sb("counts", [P, E, TT])
        tiles_of = sb("tiles_of", [P, E, 1])
        pairs_ef = sb("pairs_ef", [P, E, E])
        first_tile = sb("first_tile", [P, E, 1])
        end_tile = sb("end_tile", [P, E, 1])
        place = sb("place", [P, TT, E])
        slot_f = sb("slot_f", [P, TT])
        slot_u = sb("slot_u", [P, TT], mybir.dt.uint32)
        ended = sb("ended", [P, NS, E])
        expert_f = sb("expert_f", [P, NS])
        expert_u = sb("expert_u", [P, NS], mybir.dt.uint32)
        token_u = sb("token_u", [P, NS], mybir.dt.uint32)

        bank = ctx.enter_context(nc.psum_tensor("bank", [P, 8, N], fp32))
        SA = [bank[:, 0:2, :], bank[:, 2:4, :]]
        SB = [bank[:, 4, :], bank[:, 5, :]]
        AV = [bank[:, 6, :], bank[:, 7, :]]

        def spread_ap(ap, *dims):
            return bass.AP(ap.tensor, ap.offset, [list(ap.ap[0])] + [list(d) for d in dims])

        def bcast(ap, n):
            return bass.AP(ap.tensor, ap.offset, [list(s) for s in ap.ap][:-1] + [[0, n]])

        x_loaded = [sem(f"x_loaded{g}") for g in range(G)]
        bias_loaded = sem("bias_loaded")
        weights_loaded = sem("weights_loaded")
        moe_loaded = sem("moe_loaded")
        consts_ready = sem("consts_ready")
        pool_step = sem("pool_step")
        ones_ready = sem("ones_ready")
        sharp_ready = sem("sharp_ready")
        amp_ready = sem("amp_ready")
        bias_sq = sem("bias_sq")
        bias_exp = sem("bias_exp")
        bias_mm = sem("bias_mm")
        bias_out = sem("bias_out")
        bias_stored = sem("bias_stored")
        w_t_mm = sem("w_t_mm")
        w_t_ready = sem("w_t_ready")
        ln_stats = sem("ln_stats")
        ln_aggr = sem("ln_aggr")
        ln_std = sem("ln_std")
        ln_rstd = sem("ln_rstd")
        ln_out = sem("ln_out")
        tp_done = [sem(f"tp{a}_done") for a in range(3)]
        feat_ready = [sem(f"feat{a}_ready") for a in range(3)]
        q_mm = [sem(f"q{a}_mm") for a in range(2)]
        k_mm = [sem(f"k{a}_mm") for a in range(2)]
        v_mm = [sem(f"v{a}_mm") for a in range(2)]
        part_hi = [sem(f"part{a}_hi") for a in range(2)]
        part_rest = [sem(f"part{a}_rest") for a in range(2)]
        part_mid = [sem(f"part{a}_mid") for a in range(2)]
        part_lo = [sem(f"part{a}_lo") for a in range(2)]
        v_evac = [sem(f"v{a}_evac") for a in range(2)]
        parts_stored = [sem(f"parts{a}_stored") for a in range(2)]
        qk_loaded = [[sem(f"qk{a}_loaded{s}") for s in range(2)] for a in range(2)]
        qkb_loaded = [sem(f"qkb_loaded{s}") for s in range(2)]
        kb_minus = sem("kb_minus")
        tab_loaded = [sem(f"tab_loaded{s}") for s in range(2)]
        sa_done = [sem(f"sa{a}_done") for a in range(2)]
        max_done = [sem(f"max{a}_done") for a in range(2)]
        shift_dve = sem("shift_dve")
        shift_act = sem("shift_act")
        shift_pool = sem("shift_pool")
        sb_done = [sem(f"sb{a}_done") for a in range(2)]
        exp_done = [sem(f"exp{a}_done") for a in range(2)]
        v_ready = [sem(f"v{a}_ready") for a in range(2)]
        av_done = [sem(f"av{a}_done") for a in range(2)]
        o_ready = [sem(f"o{a}_ready") for a in range(2)]
        o_stored = [[sem(f"o{a}_stored{s}") for s in range(2)] for a in range(2)]
        split_step = sem("split_step")
        mrow_stored = sem("mrow_stored")
        mrow_loaded = [sem(f"mrow_loaded{s}") for s in range(2)]
        sums_loaded = [sem(f"sums{a}_loaded") for a in range(2)]
        heads_loaded = [sem(f"heads_loaded{g}") for g in range(G)]
        recip_done = [sem(f"recip{a}_done") for a in range(2)]
        spread_mm = [sem(f"spread{a}_mm") for a in range(2)]
        heads_scaled = [sem(f"heads{a}_scaled") for a in range(2)]
        nat_mm = [sem(f"nat{a}_mm") for a in range(2)]
        nat_ready = [sem(f"nat{a}_ready") for a in range(2)]
        x_added = sem("x_added")
        gate_mm = sem("gate_mm")
        gate_step = sem("gate_step")
        slots_ready = sem("slots_ready")
        ids_ready = sem("ids_ready")
        rank_mm = sem("rank_mm")
        route_step = sem("route_step")
        slot_known = sem("slot_known")
        expert_known = sem("expert_known")
        scattered = sem("scattered")
        slots_loaded = [sem(f"slots_loaded{q}") for q in range(NS // 4)]
        slot_t_mm = sem("slot_t_mm")
        slot_t_ready = sem("slot_t_ready")
        tokens_known = sem("tokens_known")
        w_ready = sem("w_ready")
        up_mm = sem("up_mm")
        gelu_done = sem("gelu_done")
        down_mm = sem("down_mm")
        y_ready = sem("y_ready")
        y_scattered = [sem(f"y_scattered{n}") for n in range(4)]
        y_loaded = [sem(f"y_loaded{g}") for g in range(G)]
        y_added = sem("y_added")
        out_ready = sem("out_ready")
        out_stored = sem("out_stored")
        past_wait_dve = sem("past_wait_dve")
        past_wait_pool = sem("past_wait_pool")

        SHIFT_BY = "ADADADAD"
        shift_sem = {"D": shift_dve, "A": shift_act, "P": shift_pool}

        def shift_count(i, l):
            who = SHIFT_BY[l % QB]
            per_body = 4 * SHIFT_BY.count(who)
            return i * per_body + sum(SHIFT_BY[m % QB] == who for m in range(l + 1))

        def use_of_block(u, qb):
            return u * (QB + 1) - 1 + (qb if qb < 3 else qb + 1)

        def use_of_maxima(u):
            return (u + 1) * (QB + 1) + 2

        LAST_MAXIMA = use_of_block(U, 0)
        AU = 2

        ctx.enter_context(nc.allow_non_contiguous_dma(reason="head rows and skewed tables"))
        block = ctx.enter_context(nc.Block())

        @block.sync
        def _(sp):
            for n, v in enumerate((offsets, amplitudes, sharpness)):
                sp.dma_start(bias_par[:, n, :], v.rearrange("(t h) k -> (h k) t", t=2)).then_inc(bias_loaded, 16)
            x_tiles = x.rearrange("b (t p) d -> p (b t) d", p=P)
            for g in range(G):
                sp.dma_start(x_res[:, g * TG:(g + 1) * TG, :], x_tiles[:, g * TG:(g + 1) * TG, :]).then_inc(x_loaded[g], 16)
            sp.dma_start(w_in_nat[:], w_in.rearrange("(c p) d -> p c d", p=P)).then_inc(weights_loaded, 16)
            sp.dma_start(w_qkv_sb[:], w_qkv.rearrange("d (c n) -> d c n", c=3)).then_inc(weights_loaded, 16)
            sp.dma_start(w_proj_sb[:], w_proj).then_inc(weights_loaded, 16)
            sp.dma_start(gate_w_sb[:], gate_w).then_inc(weights_loaded, 16)
            sp.dma_start(gate_b_sb[:], bass.AP(gate_b.tensor, gate_b.offset, [[0, P], [1, E]])).then_inc(weights_loaded, 16)
            for n, v in enumerate((ln1_w, ln1_b, ln2_w, ln2_b)):
                sp.dma_start(ln_par[:, n:n + 1], v.rearrange("(d o) -> d o", o=1)).then_inc(weights_loaded, 16)
            sp.wait_ge(bias_out, 4)
            sp.dma_start(bias_dram, bias_row).then_inc(bias_stored, 16)

            def store_parts(a):
                for g in range(G):
                    for s in range(2):
                        sp.wait_ge(part_lo[a], 2 * g + s + 1)
                        sp.dma_start(parts_dram[a][s, :, :, g * N:(g + 1) * N].rearrange("t p n -> p t n"),
                                     parts[:, s, :, g * N:(g + 1) * N]).then_inc(parts_stored[a], 16)
                sp.wait_ge(parts_stored[a], 16 * 2 * G)

            def rows_of(a, h, slot, q_dst, k_dst, loaded):
                for row, n, k_part in RUNS:
                    at = slice(row * DH, (row + n) * DH)
                    sp.dma_start(q_dst[at, slot, :],
                                 parts_dram[a][0, 0:n, bass.ds(h * DH, DH), :]).then_inc(loaded[slot], 16)
                    k_src = parts_dram[a][1, k_part, bass.ds(h * DH, DH), :]
                    sp.dma_start(k_dst[at, slot, :],
                                 bass.AP(k_src.tensor, k_src.offset, [[0, n], [T, DH], [1, T]])).then_inc(loaded[slot], 16)

            def table_of(h, slot):
                row = bias_dram[bass.ds(h, 1), 0:TAW]
                src = bass.AP(row.tensor, row.offset, [[1, P], [1, TAW]])
                sp.dma_start(bias_tab[:, slot, :], src).then_inc(tab_loaded[slot], 16)

            def store_unit(a, u, slot):
                sp.wait_ge(o_ready[a], u + 1)
                sp.dma_start(heads_dram[a][bass.ds(u, 1)].rearrange("o p n -> (o p) n"),
                             o_ring[:, slot, :]).then_inc(o_stored[a][slot], 16)

            def load_heads(a):
                for s in range(2):
                    sp.wait_ge(o_stored[a][s], 16 * (U // 2))
                src = heads_dram[a].rearrange("(h b) (c r) n -> h b c r n", b=B, c=4)
                dst = feat[:, :].rearrange("p (b c n) -> p b c n", b=B, c=4)
                sdst = sums[:, :].rearrange("p (b c n) -> p b c n", b=B, c=4)
                for b in range(B):
                    sp.dma_start(sdst[:, b], src[:, b, :, DH, :]).then_inc(sums_loaded[a], 16)
                for b in range(B):
                    for c in range(4):
                        sp.dma_start(dst[:, b, c], src[:, b, c, 0:DH, :]).then_inc(heads_loaded[b * 2 + c // 2], 16)

            store_parts(0)
            sp.wait_ge(bias_stored, 16)
            sp.wait_ge(ones_ready, 1)
            for h in range(2):
                rows_of(0, h, h, q_rows, k_rows, qk_loaded[0])
                table_of(h, h)
            sp.dma_start(w_moe[:, :, 0:HID], w1.rearrange("e d n -> d e n")).then_inc(moe_loaded, 16)
            for e in range(E):
                sp.dma_start(w_moe[:, e, HID:2 * HID].rearrange("p (c d) -> p c d", c=HC),
                             w2[e].rearrange("(c p) d -> p c d", p=P)).then_inc(moe_loaded, 16)
            slot_tiles = slots_dram.rearrange("(j p) c -> p j c", p=P)
            sp.dma_start(slot_tiles[:, :, 0:D], spread_ap(zeros[:, :], [0, NS], [1, D])).then_inc(slots_ready, 16)
            sp.dma_start(slot_tiles[:, :, D:RW], spare_no[:, :].rearrange("p (j o) -> p j o", o=1)).then_inc(slots_ready, 16)

            def pair1(i, first=False, last=False):
                for hl in range(2):
                    h = 2 * i + hl
                    if not (first and hl == 0):
                        for b in range(B):
                            store_unit(0, 2 * h - 2 + b, b)
                    if not last:
                        sp.wait_ge(sa_done[0], QB * B * (h + 1))
                        rows_of(0, h + 2, hl, q_rows, k_rows, qk_loaded[0])
                        sp.wait_ge(max_done[0], QB * B * (h + 1))
                        table_of(h + 2, hl)

            pair1(0, first=True)
            with sp.Fori(1, PAIRS - 1) as i:
                pair1(i)
            pair1(PAIRS - 1, last=True)
            for b in range(B):
                store_unit(0, U - 2 + b, b)
            load_heads(0)

            store_parts(1)
            sp.wait_ge(kb_minus, 4)
            for h in range(2):
                rows_of(1, h, h, q_rows, k_rows, qk_loaded[1])
            for h in range(2):
                rows_of(1, h, h, qb_rows, kb_rows, qkb_loaded)

            def maxima_of(u, slot, use, count_first=False):
                sp.wait_ge(max_done[1], use + 1)
                head_slot, b = (slot // B) % 2, slot % B
                sp.dma_start(maxima_dram[slot % 2], max_rows[:, slot % 2, :]).then_inc(mrow_stored, 16)
                sp.wait_ge(mrow_stored, 16 * (u + 1))
                sp.dma_start(qb_rows[KR:KR + 3, head_slot, b * L:(b + 1) * L],
                             maxima_dram[slot % 2].rearrange("(p q) c -> p (q c)", p=3)).then_inc(mrow_loaded[slot % 2], 16)

            maxima_of(0, 0, use_of_maxima(0))

            def pair2(i, first=False, last=False):
                for ul in range(4):
                    u = 4 * i + ul
                    if not (last and ul == 3):
                        use = LAST_MAXIMA if last and ul == 2 else use_of_maxima(u + 1)
                        maxima_of(u + 1, (ul + 1) % 4, use)
                    if ul % 2 == 0:
                        hb = 2 * i + ul // 2 + 1
                        slot = (ul // 2 + 1) % 2
                        if not (first and ul == 0):
                            sp.wait_ge(sb_done[1], 2 * QB * u)
                            if not (last and ul == 2):
                                rows_of(1, hb, slot, qb_rows, kb_rows, qkb_loaded)
                        if not last:
                            sp.wait_ge(sa_done[1], use_of_block(u + AU - 1, QB - 1) + 1)
                            rows_of(1, hb + 1, 1 - slot, q_rows, k_rows, qk_loaded[1])
                    if not (first and ul == 0):
                        store_unit(1, u - 1, (ul - 1) % 2)

            pair2(0, first=True)
            with sp.Fori(1, PAIRS - 1) as i:
                pair2(i)
            pair2(PAIRS - 1, last=True)
            store_unit(1, U - 1, (U - 1) % 2)
            load_heads(1)

            sp.wait_ge(scattered, 16 * TT)
            for q in range(NS // 4):
                sp.dma_start(slot_rows[:, 4 * q:4 * q + 4, :], slot_tiles[:, 4 * q:4 * q + 4, :]).then_inc(slots_loaded[q], 16)
            for n in range(4):
                sp.wait_ge(y_scattered[n], 16 * (NS // 4))
            moe_tiles = moe_dram[0:T].rearrange("(t p) d -> p t d", p=P)
            for g in range(G):
                sp.dma_start(norm[:, g * TG:(g + 1) * TG, :], moe_tiles[:, g * TG:(g + 1) * TG, :]).then_inc(y_loaded[g], 16)

            out_tiles = out.rearrange("b (t p) d -> p (b t) d", p=P)
            for g in range(G):
                sp.wait_ge(out_ready, g + 1)
                sp.dma_start(out_tiles[:, g * TG:(g + 1) * TG, :], norm[:, g * TG:(g + 1) * TG, :]).then_inc(out_stored, 16)
            sp.wait_ge(out_stored, 16 * G)

        @block.gpsimd
        def _(pool):
            steps = [0]

            def chain(ins):
                steps[0] += 1
                ins.then_inc(pool_step, 1)
                pool.wait_ge(pool_step, steps[0])

            nc.gpsimd.iota(rel_pos, [[-1, 2 * L]], base=L - 1, channel_multiplier=0,
                           allow_small_or_imprecise_dtypes=True).then_inc(consts_ready, 1)
            chain(nc.gpsimd.memset(amp_sel[:], 1.0))
            chain(nc.gpsimd.affine_select(out=amp_sel[:], in_=amp_sel[:], compare_op=ALU.is_ge, fill=0.0, base=0,
                                          pattern=[[P, 2], [-NK, H]], channel_multiplier=1))
            chain(nc.gpsimd.affine_select(out=amp_sel[:], in_=amp_sel[:], compare_op=ALU.is_ge, fill=0.0,
                                          base=NK - 1, pattern=[[-P, 2], [NK, H]], channel_multiplier=-1))
            nc.gpsimd.memset(eps_col[:], EPS).then_inc(consts_ready, 1)
            chain(nc.gpsimd.memset(ident[:], 0.0))
            chain(nc.gpsimd.affine_select(out=ident[:], in_=ident[:], compare_op=ALU.not_equal, fill=1.0, base=0,
                                          pattern=[[-1, P]], channel_multiplier=1))
            chain(nc.gpsimd.tensor_copy(ident_b[:], ident[:]))
            chain(nc.gpsimd.memset(head_sel[:], 1.0))
            chain(nc.gpsimd.affine_select(out=head_sel[:], in_=head_sel[:], compare_op=ALU.is_ge, fill=0.0, base=0,
                                          pattern=[[1, D]], channel_multiplier=-DH))
            chain(nc.gpsimd.affine_select(out=head_sel[:], in_=head_sel[:], compare_op=ALU.is_ge, fill=0.0,
                                          base=DH - 1, pattern=[[-1, D]], channel_multiplier=DH))
            nc.gpsimd.iota(order[:], [[-1, E]], base=E, channel_multiplier=0,
                           allow_small_or_imprecise_dtypes=True).then_inc(consts_ready, 1)
            pool.wait_ge(consts_ready, 3)
            chain(nc.gpsimd.memset(onehot[:], 0.0))
            chain(nc.gpsimd.memset(zeros[:], 0.0))
            chain(nc.gpsimd.memset(ones_b[:], 1.0))
            chain(nc.gpsimd.affine_select(out=before[:], in_=ones_b[:], compare_op=ALU.is_gt, fill=0.0, base=0,
                                          pattern=[[1, P]], channel_multiplier=-1))
            chain(nc.gpsimd.memset(lower[:], 1.0))
            chain(nc.gpsimd.affine_select(out=lower[:], in_=lower[:], compare_op=ALU.is_gt, fill=0.0, base=0,
                                          pattern=[[1, E], [-1, E]], channel_multiplier=0))
            for dst, pattern, base, per_row in ((steps_of_tile, [[P, TT]], 0, 0), (tile_no, [[1, NS]], 0, 0),
                                                (token_no, [[P, TT]], 0, 1), (spare_no, [[P, NS]], T, 1)):
                chain(nc.gpsimd.iota(dst[:], pattern, base=base, channel_multiplier=per_row,
                                     allow_small_or_imprecise_dtypes=True))
            for rows in (q_rows, k_rows):
                chain(nc.gpsimd.memset(rows[32:64], 0.0))
                chain(nc.gpsimd.memset(rows[64:P], 0.0))
            chain(nc.gpsimd.memset(v_ring[:], 0.0))
            chain(nc.gpsimd.memset(v_ring[:, :, :, DH:DH + 1], 1.0))
            pool.sem_inc(ones_ready, 1)

            def v_of(a, h, slot, wait):
                if wait:
                    pool.wait_ge(av_done[a], B * (h - 1))
                pool.sem_inc(past_wait_pool, 1)
                nc.gpsimd.tensor_copy(v_ring[:, slot, :, 0:DH],
                                      v_nat[:, :, bass.ds(h * DH, DH)]).then_inc(v_ready[a], 1)

            pool.wait_ge(v_evac[0], G)
            def pair1(i, first=False):
                for l in range(4 * QB):
                    if l % (2 * QB) == 0:
                        v_of(0, 2 * i + l // (2 * QB), l // (2 * QB), not first)
                    if SHIFT_BY[l % QB] == "P":
                        pool.wait_ge(max_done[0], 4 * QB * i + l + 1)
                        t = logit[:, l % NT, :]
                        nc.gpsimd.tensor_tensor(t, t, bcast(row_max[:, l % QB:l % QB + 1], L),
                                                ALU.subtract).then_inc(shift_pool, 1)

            pair1(0, first=True)
            with pool.Fori(1, PAIRS) as i:
                pair1(i)

            pool.wait_ge(max_done[0], QB * U)
            pool.wait_ge(shift_pool, 4 * SHIFT_BY.count("P") * PAIRS)
            pool.wait_ge(v_ready[0], H)
            nc.gpsimd.memset(kb_rows[32:64], -1.0).then_inc(kb_minus, 1)
            pool.wait_ge(kb_minus, 1)
            nc.gpsimd.memset(kb_rows[64:P], 0.0).then_inc(kb_minus, 1)
            nc.gpsimd.memset(qb_rows[64:P], 0.0).then_inc(kb_minus, 1)
            pool.wait_ge(kb_minus, 3)
            nc.gpsimd.memset(qb_rows[32:64], 0.0).then_inc(kb_minus, 1)
            pool.wait_ge(kb_minus, 4)

            def split_maxima(u, slot):
                pool.wait_ge(max_done[1], use_of_block(u, QB - 1) + 1 if not isinstance(u, int) or u else QB)
                m, r = unit_max[:, slot, :], max_rest[:, slot]
                hi, mid, lo = (max_parts[:, slot, n * QB:(n + 1) * QB] for n in range(3))
                pool.sem_inc(past_wait_pool, 1)
                nc.gpsimd.tensor_copy(hi, m).then_inc(split_step, 1)
                pool.wait_ge(split_step, 4 * u + 1)
                nc.gpsimd.tensor_tensor(r[:, 0, :], m, hi, ALU.subtract).then_inc(split_step, 1)
                pool.wait_ge(split_step, 4 * u + 2)
                pool.sem_inc(past_wait_pool, 1)
                nc.gpsimd.tensor_copy(mid, r[:, 0, :]).then_inc(split_step, 1)
                pool.wait_ge(split_step, 4 * u + 3)
                nc.gpsimd.tensor_tensor(lo, r[:, 0, :], mid, ALU.subtract).then_inc(split_step, 1)

            pool.wait_ge(v_evac[1], G)
            pool.wait_ge(av_done[0], U)
            split_maxima(0, 0)
            split_maxima(1, 1)

            def pair2(i, first=False, last=False):
                for ul in range(4):
                    if ul % 2 == 0:
                        v_of(1, 2 * i + ul // 2, ul // 2, not first)
                    if not (last and ul >= 2):
                        split_maxima(4 * i + ul + AU, ul % 2)

            pair2(0, first=True)
            with pool.Fori(1, PAIRS - 1) as i:
                pair2(i)
            pair2(PAIRS - 1, last=True)

            pool.wait_ge(slots_ready, 32)
            pool.wait_ge(ln_out, 5 * TT)
            pool.wait_ge(ids_ready, 1)
            pool.wait_ge(slot_known, 1)
            for t in range(TT):
                nc.gpsimd.indirect_dma_start(out=slots_dram, out_offset=bass.IndirectOffsetOnAxis(ap=slot_u[:, t:t + 1], axis=0),
                                             in_=token_rows[:, t, :], in_offset=None).then_inc(scattered, 16)
            for j in range(NS):
                if j == 0:
                    pool.wait_ge(tokens_known, 1)
                pool.wait_ge(y_ready, j + 1)
                nc.gpsimd.indirect_dma_start(out=moe_dram, out_offset=bass.IndirectOffsetOnAxis(ap=token_u[:, j:j + 1], axis=0),
                                             in_=y_ring[:, j % 4, :], in_offset=None).then_inc(y_scattered[j % 4], 16)

        @block.scalar
        def _(act):
            act.wait_ge(consts_ready, 1)
            act.wait_ge(bias_loaded, 48)
            for t in range(2):
                nc.scalar.activation(bias_e[:, t, :], rel_pos, ACT.Square, bias=bias_par[:, 0, t:t + 1]).then_inc(bias_sq, 1)
            act.wait_ge(sharp_ready, 2)
            for t in range(2):
                act.wait_ge(bias_sq, t + 1)
                nc.scalar.activation(bias_e[:, t, :], bias_e[:, t, :], ACT.Exp,
                                     scale=neg_sharp[:, t:t + 1]).then_inc(bias_exp, 1)
            act.wait_ge(w_t_mm, 1)
            nc.scalar.copy(w_in_t[:].rearrange("p c d -> p (c d)"), bank[:, 4, 0:3 * D]).then_inc(w_t_ready, 1)

            def norm_std(n):
                for g in range(G):
                    act.wait_ge(ln_aggr, n * TT + TG * (g + 1))
                    ts = slice(g * TG, (g + 1) * TG)
                    nc.scalar.activation(std[:, ts], meanvar[:, ts, 1], ACT.Sqrt, bias=eps_col[:, 0:1]).then_inc(ln_std, 1)

            def feature_major(a, par):
                for g in range(G):
                    act.wait_ge(tp_done[a], g + 1)
                    dst, src = feat[:, g * N:(g + 1) * N], bank[:, g, :]
                    if par is None:
                        nc.scalar.copy(dst, src).then_inc(feat_ready[a], 1)
                    else:
                        nc.scalar.activation(dst, src, ACT.Identity, scale=ln_par[:, par:par + 1],
                                             bias=ln_par[:, par + 1:par + 2]).then_inc(feat_ready[a], 1)

            def projections(a):
                for g in range(G):
                    cols = slice(g * N, (g + 1) * N)
                    act.wait_ge(q_mm[a], g + 1)
                    nc.scalar.activation(parts[:, 0, 0, cols], bank[:, 4, :], ACT.Copy, scale=SCALE).then_inc(part_hi[a], 1)
                    act.wait_ge(k_mm[a], g + 1)
                    nc.scalar.copy(parts[:, 1, 0, cols], bank[:, 5, :]).then_inc(part_hi[a], 1)
                    act.wait_ge(v_mm[a], g + 1)
                    nc.scalar.copy(v_nat[:, g * TG:(g + 1) * TG, :],
                                   bank[:, 6, :].rearrange("p (t d) -> p t d", t=TG)).then_inc(v_evac[a], 1)
                    for s in range(2):
                        act.wait_ge(part_rest[a], 2 * g + s + 1)
                        nc.scalar.copy(parts[:, s, 1, cols], rest[:, s, :]).then_inc(part_mid[a], 1)

            def evacuate(a, u, slot, wait):
                act.wait_ge(av_done[a], u + 1)
                if wait:
                    act.wait_ge(o_stored[a][slot], 8 * (u - slot))
                nc.scalar.copy(o_ring[:, slot, :], AV[slot][:, 0:L // 4]).then_inc(o_ready[a], 1)

            norm_std(0)
            feature_major(0, None)
            projections(0)

            def shift(i, l):
                if SHIFT_BY[l % QB] == "A":
                    act.wait_ge(max_done[0], 4 * QB * i + l + 1)
                    t = logit[:, l % NT, :]
                    nc.scalar.activation(t, t, ACT.Identity, scale=-1.0,
                                         bias=row_max[:, l % QB:l % QB + 1]).then_inc(shift_act, 1)

            def pair1(i, first=False, last=False):
                for l in range(4 * QB):
                    ul, qb = l // QB, l % QB
                    if qb == 1 and not (first and ul < 2):
                        evacuate(0, 4 * i + ul - 2, ul % 2, not (first and ul < 4))
                    if qb == 0 and not (first and ul < 2):
                        act.wait_ge(av_done[0], 4 * i + ul - 1)
                    for j in range(2):
                        act.wait_ge(sb_done[0], 8 * QB * i + 2 * l + j + 1)
                        nc.scalar.activation(prob[:, ul % 2, 4 * j:4 * j + 4, qb * P:(qb + 1) * P],
                                             SB[j].rearrange("p (k q) -> p k q", k=4), ACT.Exp,
                                             scale=-1.0 if SHIFT_BY[qb] == "A" else 1.0).then_inc(exp_done[0], 1)
                    if not (last and l + 2 >= 4 * QB):
                        shift(i, l + 2)

            for l in range(2):
                shift(0, l)
            pair1(0, first=True)
            with act.Fori(1, PAIRS - 1) as i:
                pair1(i)
            pair1(PAIRS - 1, last=True)
            for u in (U - 2, U - 1):
                evacuate(0, u, u % 2, True)

            for g in range(G):
                act.wait_ge(nat_mm[0], g + 1)
                nc.scalar.copy(norm[:, g * TG:(g + 1) * TG, :],
                               bank[:, 4 + g, :].rearrange("p (t d) -> p t d", t=TG)).then_inc(nat_ready[0], 1)
            norm_std(1)
            norm_std(2)
            norm_std(3)
            feature_major(1, 0)
            projections(1)

            def pair2(i, first=False, last=False):
                for ul in range(4):
                    u = 4 * i + ul
                    if not (first and ul < 2):
                        act.wait_ge(av_done[1], u - 1)
                    for kb in range(QB):
                        if kb == 3 and not (first and ul < 1):
                            evacuate(1, u - 1, (ul - 1) % 2, not (first and ul < 3))
                        for half in range(2):
                            act.wait_ge(sb_done[1], 8 * QB * i + 2 * (QB * ul + kb) + half + 1)
                            nc.scalar.activation(prob[:, ul % 2, kb, half * N:(half + 1) * N], SB[half],
                                                 ACT.Exp).then_inc(exp_done[1], 1)

            pair2(0, first=True)
            with act.Fori(1, PAIRS) as i:
                pair2(i)
            evacuate(1, U - 1, (U - 1) % 2, True)

            norm_std(4)
            feature_major(2, 2)
            for q in range(NS // 4):
                act.wait_ge(slot_t_mm, q + 1)
                nc.scalar.activation(slot_feat[:, q * N:(q + 1) * N], bank[:, q % 2, :], ACT.Identity,
                                     scale=ln_par[:, 2:3], bias=ln_par[:, 3:4]).then_inc(slot_t_ready, 1)

            def four_tiles(i, first=False):
                for n in range(4):
                    j = 4 * i + n
                    act.wait_ge(up_mm, j + 1)
                    if not (first and n < 2):
                        act.wait_ge(down_mm, j - 1)
                    nc.scalar.activation(hidden[:, n % 2, :, :], bank[:, 2 + n % 2, :].rearrange("p (c n) -> p c n", c=HC),
                                         ACT.Gelu_apprx_tanh).then_inc(gelu_done, 1)

            four_tiles(0, first=True)
            with act.Fori(1, NS // 4) as i:
                four_tiles(i)
            norm_std(5)

        @block.vector
        def _(dve):
            dve.wait_ge(bias_loaded, 48)
            nc.vector.tensor_scalar(neg_sharp[:], bias_par[:, 2, :], -1.0, None, ALU.mult).then_inc(sharp_ready, 1)
            dve.wait_ge(sharp_ready, 1)
            nc.vector.tensor_tensor(neg_sharp[:], neg_sharp[:], bias_par[:, 2, :], ALU.min).then_inc(sharp_ready, 1)

            def norm_stats(n, src, wait):
                for t in range(TT):
                    if t % TG == 0:
                        wait(t // TG)
                    nc.vector.bn_stats(stats[:, t, :], src[:, t, :]).then_inc(ln_stats, 1)
                for t in range(TT):
                    dve.wait_ge(ln_stats, n * TT + t + 1)
                    nc.vector.bn_aggr(meanvar[:, t, :], stats[:, t, :]).then_inc(ln_aggr, 1)

            def norm_apply(n, src, dst, then=None):
                for g in range(G):
                    ts = slice(g * TG, (g + 1) * TG)
                    dve.wait_ge(ln_std, n * G + g + 1)
                    nc.vector.reciprocal(rstd[:, ts], std[:, ts]).then_inc(ln_rstd, 1)
                    dve.wait_ge(ln_rstd, n * G + g + 1)
                    for t in range(g * TG, (g + 1) * TG):
                        nc.vector.tensor_scalar(dst[:, t, :], src[:, t, :], meanvar[:, t, 0:1], rstd[:, t:t + 1],
                                                ALU.subtract, ALU.mult).then_inc(ln_out, 1)
                    if then:
                        dve.wait_ge(ln_out, n * TT + TG * (g + 1))
                        then(g, ts)

            norm_stats(0, x_res, lambda g: dve.wait_ge(x_loaded[g], 16))
            norm_apply(0, x_res, norm)
            dve.wait_ge(ones_ready, 1)
            for t in range(2):
                ins = nc.vector.tensor_scalar(amp_sel[:, t, :], amp_sel[:, t, :], bias_par[:, 1, t:t + 1], None, ALU.mult)
            ins.then_inc(amp_ready, 1)
            for c in range(4):
                dve.wait_ge(bias_mm, c + 1)
                nc.vector.tensor_copy(bias_row[:, c * N:(c + 1) * N], bank[0:H, c, :]).then_inc(bias_out, 1)

            def projections(a):
                for g in range(G):
                    cols = slice(g * N, (g + 1) * N)
                    for s in range(2):
                        dve.wait_ge(part_hi[a], 2 * g + s + 1)
                        if g:
                            dve.wait_ge(part_lo[a], 2 * (g - 1) + s + 1)
                        nc.vector.scalar_tensor_tensor(rest[:, s, :], bank[:, 4 + s, :], SCALE if s == 0 else 1.0,
                                                       parts[:, s, 0, cols], ALU.mult, ALU.subtract).then_inc(part_rest[a], 1)
                    for s in range(2):
                        dve.wait_ge(part_mid[a], 2 * g + s + 1)
                        nc.vector.tensor_tensor(parts[:, s, 2, cols], rest[:, s, :], parts[:, s, 1, cols],
                                                ALU.subtract).then_inc(part_lo[a], 1)

            projections(0)

            def shift(i, l):
                if SHIFT_BY[l % QB] == "D":
                    dve.wait_ge(max_done[0], 4 * QB * i + l + 1)
                    t = logit[:, l % NT, :]
                    nc.vector.tensor_scalar(t, t, row_max[:, l % QB:l % QB + 1], None, ALU.subtract).then_inc(shift_dve, 1)

            def pair1(i, first=False):
                for l in range(4 * QB):
                    s, qb = 4 * QB * i + l, l % QB
                    head_slot = l // (2 * QB)
                    if l % (2 * QB) == 0:
                        dve.wait_ge(tab_loaded[head_slot], 16 * (i + 1))
                    dve.wait_ge(sa_done[0], s + 1)
                    if not (first and l < NT):
                        dve.wait_ge(sb_done[0], 2 * (s - NT) + 2)
                    dve.sem_inc(past_wait_dve, 1)
                    tab = bias_tab[:, head_slot, qb * P + L - 1:qb * P + L]
                    bias = bass.AP(tab.tensor, tab.offset, [list(tab.ap[0]), [-1, L]])
                    nc.vector.tensor_tensor_reduce(
                        out=logit[:, l % NT, :], in0=SA[l % 2].rearrange("p a n -> p (a n)"), in1=bias,
                        scale=1.0, scalar=LEAST, op0=ALU.add, op1=ALU.max,
                        accum_out=row_max[:, qb:qb + 1]).then_inc(max_done[0], 1)
                    if l:
                        shift(i, l - 1)
                    if l == 4 * QB - 1:
                        shift(i, l)
                pass

            pair1(0, first=True)
            with dve.Fori(1, PAIRS) as i:
                pair1(i)

            def scale_heads(a):
                dve.wait_ge(sums_loaded[a], 16 * B)
                for g in range(G):
                    cols = slice(g * N, (g + 1) * N)
                    nc.vector.reciprocal(sums[:, cols], sums[:, cols]).then_inc(recip_done[a], 1)
                for g in range(G):
                    cols = slice(g * N, (g + 1) * N)
                    dve.wait_ge(heads_loaded[g], 32 * (a + 1))
                    dve.wait_ge(spread_mm[a], g + 1)
                    nc.vector.tensor_tensor(feat[:, cols], feat[:, cols], bank[:, g, :], ALU.mult).then_inc(heads_scaled[a], 1)

            scale_heads(0)
            norm_stats(1, norm, lambda g: dve.wait_ge(nat_ready[0], g + 1))

            def add_x(g, ts):
                nc.vector.tensor_tensor(x_res[:, ts, :], x_res[:, ts, :], norm[:, ts, :], ALU.add).then_inc(x_added, 1)

            norm_apply(1, norm, norm, add_x)
            norm_stats(2, x_res, lambda g: dve.wait_ge(x_added, g + 1))
            norm_apply(2, x_res, y_res)
            norm_stats(3, y_res, lambda g: dve.wait_ge(ln_out, 2 * TT + TG * (g + 1)))
            norm_apply(3, y_res, norm)
            projections(1)

            def block_max(u, qb, use, slot):
                dve.wait_ge(sa_done[1], use + 1)
                nc.vector.tensor_reduce(unit_max[:, slot, qb:qb + 1], SA[use_parity[0]].rearrange("p a n -> p (a n)"),
                                        AX.X, ALU.max).then_inc(max_done[1], 1)

            use_parity = [0]

            def maxima_out(use, parity, slot, stored):
                dve.wait_ge(sa_done[1], use + 1)
                if stored is not None:
                    dve.wait_ge(mrow_stored, 16 * stored)
                nc.vector.tensor_copy(max_rows[:, slot, :],
                                      SA[parity][0:3 * QB, 0, 0:P // 2].bitcast(bf16)).then_inc(max_done[1], 1)

            for qb in range(QB):
                use_parity[0] = qb % 2
                block_max(0, qb, qb, 0)
            for qb in range(QB):
                use_parity[0] = use_of_block(1, qb) % 2
                block_max(1, qb, use_of_block(1, qb), 1)
                if qb == 2:
                    maxima_out(use_of_maxima(0), use_of_maxima(0) % 2, 0, None)

            def pair2(i, first=False, last=False):
                for ul in range(4):
                    u, lu = 4 * i + ul, ul + AU
                    done = last and ul >= 2
                    for qb in range(QB):
                        if not done:
                            use_parity[0] = use_of_block(lu, qb) % 2
                            block_max(u + AU, qb, use_of_block(u + AU, qb), ul % 2)
                        if qb == 2 and not (last and ul == 3):
                            use = LAST_MAXIMA if done else use_of_maxima(u + 1)
                            parity = (LAST_MAXIMA if done else use_of_maxima(lu - 1)) % 2
                            maxima_out(use, parity, (ul + 1) % 2, None if first and ul == 0 else u)

            pair2(0, first=True)
            with dve.Fori(1, PAIRS - 1) as i:
                pair2(i)
            pair2(PAIRS - 1, last=True)

            scale_heads(1)
            for g in range(G):
                ts = slice(g * TG, (g + 1) * TG)
                dve.wait_ge(nat_mm[1], g + 1)
                nc.vector.tensor_tensor(y_res[:, ts, :], y_res[:, ts, :],
                                        bank[:, 4 + g, :].rearrange("p (t d) -> p t d", t=TG), ALU.add).then_inc(nat_ready[1], 1)
            norm_stats(4, y_res, lambda g: dve.wait_ge(nat_ready[1], g + 1))
            norm_apply(4, y_res, token_rows[:, :, 0:D])
            nc.vector.tensor_copy(token_rows[:, :, D:RW], token_no[:, :].rearrange("p (t o) -> p t o", o=1)).then_inc(ids_ready, 1)

            n = [0]

            def chain(ins):
                n[0] += 1
                ins.then_inc(gate_step, 1)
                dve.wait_ge(gate_step, n[0])

            dve.wait_ge(gate_mm, 1)
            dve.wait_ge(weights_loaded, 16 * 9)
            gate_b_all = spread_ap(gate_b_sb[:, :], [0, TT], [1, E])
            order_all = spread_ap(order[:, :], [0, TT], [1, E])
            max_all = spread_ap(gate_max[:, :, :], [1, TT], [0, E])
            hot = onehot[:, 0:TT, :]
            chain(nc.vector.tensor_tensor(gate[:], bank[:, 7, 0:TT * E].rearrange("p (t e) -> p t e", t=TT), gate_b_all, ALU.add))
            chain(nc.vector.tensor_reduce(gate_max[:], gate[:], AX.X, ALU.max))
            chain(nc.vector.tensor_tensor(hot, gate[:], max_all, ALU.is_equal))
            chain(nc.vector.tensor_tensor(gate[:], hot, order_all, ALU.mult))
            chain(nc.vector.tensor_reduce(gate_max[:], gate[:], AX.X, ALU.max))
            chain(nc.vector.tensor_tensor(hot, gate[:], max_all, ALU.is_equal))

            dve.wait_ge(rank_mm, 1)
            rank = bank[:, 6, 0:(TT + 1) * E].rearrange("p (t e) -> p t e", e=E)
            chain(nc.vector.tensor_copy(end_tile[:], rank[:, TT, :].rearrange("p (e o) -> p e o", o=1)))
            chain(nc.vector.tensor_tensor(counts[:], spread_ap(end_tile[:, :, :], [1, E], [0, TT]),
                                          spread_ap(steps_of_tile[:, :], [0, E], [1, TT]), ALU.is_gt))
            chain(nc.vector.tensor_reduce(tiles_of[:], counts[:], AX.X, ALU.add))
            chain(nc.vector.tensor_tensor(pairs_ef[:], lower[:], spread_ap(tiles_of[:, :, :], [0, E], [1, E]), ALU.mult))
            chain(nc.vector.tensor_reduce(first_tile[:], pairs_ef[:], AX.X, ALU.add))
            chain(nc.vector.scalar_tensor_tensor(place[:], spread_ap(first_tile[:, :, :], [0, TT], [1, E]), float(P),
                                                 rank[:, 0:TT, :], ALU.mult, ALU.add))
            chain(nc.vector.tensor_tensor(place[:], place[:], hot, ALU.mult))
            chain(nc.vector.tensor_reduce(slot_f[:], place[:], AX.X, ALU.add))
            nc.vector.tensor_copy(slot_u[:], slot_f[:]).then_inc(slot_known, 1)
            chain(nc.vector.tensor_tensor(end_tile[:], first_tile[:], tiles_of[:], ALU.add))
            chain(nc.vector.tensor_tensor(ended[:], spread_ap(end_tile[:, :, :], [0, NS], [1, E]),
                                          spread_ap(tile_no[:, :], [1, NS], [0, E]), ALU.is_le))
            chain(nc.vector.tensor_reduce(expert_f[:], ended[:], AX.X, ALU.add))
            chain(nc.vector.tensor_scalar(expert_f[:], expert_f[:], float(E - 1), None, ALU.min))
            nc.vector.tensor_copy(expert_u[:], expert_f[:]).then_inc(expert_known, 1)
            dve.wait_ge(expert_known, 1)
            dve.wait_ge(moe_loaded, 16 * (1 + E))

            def weights(i, n, first):
                j = 4 * i + n
                e = dve.value_load(expert_u[0:1, bass.ds(j, 1)], min_val=0, max_val=E - 1)
                if not first:
                    dve.wait_ge(down_mm, j - 3)
                    dve.sem_inc(past_wait_dve, 1)
                nc.vector.tensor_copy(w_ring[:, n, :], w_moe[:, bass.ds(e, 1), :].rearrange("p o w -> p (o w)")).then_inc(w_ready, 1)

            def result(i, n, first):
                j = 4 * i + n
                dve.wait_ge(down_mm, j + 1)
                if not first:
                    dve.wait_ge(y_scattered[n], 16 * i)
                nc.vector.tensor_copy(y_ring[:, n, :], bank[:, 4 + n % 2, 0:D]).then_inc(y_ready, 1)

            for n in range(3):
                weights(0, n, True)
            for q in range(NS // 4):
                dve.wait_ge(slots_loaded[q], 16)
            nc.vector.tensor_copy(token_u[:], slot_rows[:, :, D]).then_inc(tokens_known, 1)

            def four_tiles(i, first=False, last=False):
                for n in range(4):
                    if n == 0:
                        weights(i, 3, first)
                    elif not last:
                        weights(i + 1, n - 1, False)
                    result(i, n, first)

            four_tiles(0, first=True)
            with dve.Fori(1, NS // 4 - 1) as i:
                four_tiles(i)
            four_tiles(NS // 4 - 1, last=True)
            for g in range(G):
                ts = slice(g * TG, (g + 1) * TG)
                dve.wait_ge(y_loaded[g], 16)
                nc.vector.tensor_tensor(y_res[:, ts, :], y_res[:, ts, :], norm[:, ts, :], ALU.add).then_inc(y_added, 1)

            norm_stats(5, y_res, lambda g: dve.wait_ge(y_added, g + 1))

            def add_out(g, ts):
                nc.vector.tensor_tensor(norm[:, ts, :], x_res[:, ts, :], norm[:, ts, :], ALU.add).then_inc(out_ready, 1)

            norm_apply(5, y_res, norm, add_out)

        @block.tensor
        def _(pe):
            pe.wait_ge(ones_ready, 1)
            pe.wait_ge(weights_loaded, 16 * 9)
            for c in range(3):
                ins = nc.tensor.transpose(bank[:, 4, c * D:(c + 1) * D], w_in_nat[:, c, :], ident[:])
            ins.then_inc(w_t_mm, 1)
            pe.wait_ge(amp_ready, 1)
            pe.wait_ge(bias_exp, 2)
            for c in range(4):
                for t in range(2):
                    ins = nc.tensor.matmul(bank[0:H, c, :], amp_sel[:, t, :], bias_e[:, t, c * N:(c + 1) * N],
                                           start=(t == 0), stop=(t == 1))
                ins.then_inc(bias_mm, 1)

            def transposes(a, ln, src=norm):
                for g in range(G):
                    pe.wait_ge(ln_out, ln * TT + TG * (g + 1))
                    for tt in range(TG):
                        ins = nc.tensor.transpose(bank[:, g, tt * P:(tt + 1) * P], src[:, g * TG + tt, :], ident[:])
                    ins.then_inc(tp_done[a], 1)

            def projections(a, wq, wk, wv):
                for g in range(G):
                    cols = slice(g * N, (g + 1) * N)
                    pe.wait_ge(feat_ready[a], g + 1)
                    if g:
                        pe.wait_ge(part_rest[a], 2 * g - 1)
                    nc.tensor.matmul(bank[:, 4, :], wq, feat[:, cols], start=True, stop=True).then_inc(q_mm[a], 1)
                    if g:
                        pe.wait_ge(part_rest[a], 2 * g)
                    nc.tensor.matmul(bank[:, 5, :], wk, feat[:, cols], start=True, stop=True).then_inc(k_mm[a], 1)
                    if g:
                        pe.wait_ge(v_evac[a], g)
                    for tt in range(TG):
                        t = g * TG + tt
                        ins = nc.tensor.matmul(bank[:, 6, tt * P:(tt + 1) * P], feat[:, t * P:(t + 1) * P], wv,
                                               start=True, stop=True)
                    ins.then_inc(v_mm[a], 1)

            pe.wait_ge(bias_out, 4)
            pe.wait_ge(w_t_ready, 1)
            transposes(0, 0)
            projections(0, w_in_t[:, 2, :], w_in_t[:, 0, :], w_in_t[:, 1, :])

            def scores_a(slot, head_slot, b, qb, sem_done):
                lhs = q_rows[:, head_slot, b * L + qb * P:b * L + (qb + 1) * P]
                for j in range(2):
                    ins = nc.tensor.matmul(SA[slot][:, j, :], lhs,
                                           k_rows[:, head_slot, b * L + j * N:b * L + (j + 1) * N], start=True, stop=True)
                ins.then_inc(sem_done, 1)

            def weigh_v(a, ul, kb, last_inc):
                head_slot, b = (ul // B) % 2, ul % B
                W = L // 4
                for c in range(4):
                    ins = nc.tensor.matmul(AV[ul % 2][VM * c:VM * (c + 1), 0:W], v_ring[:, head_slot, b * QB + kb, :],
                                           prob[:, ul % 2, kb, c * W:(c + 1) * W], start=(kb == 0), stop=(kb == QB - 1),
                                           tile_position=(0, VM * c))
                if last_inc:
                    ins.then_inc(av_done[a], 1)

            def before_av(a, i, ul, guard_bank):
                u = 4 * i + ul
                if ul % 2 == 0:
                    pe.wait_ge(v_ready[a], 2 * i + ul // 2 + 1)
                if guard_bank:
                    pe.wait_ge(o_ready[a], u - 1)

            pe.wait_ge(part_rest[0], 2 * G)
            pe.wait_ge(v_evac[0], G)

            def block_a(i, l, first):
                s = 4 * QB * i + l
                ul, qb = l // QB, l % QB
                if l % (2 * QB) == 0:
                    pe.wait_ge(qk_loaded[0][(ul // B) % 2], 16 * QK_DMAS * (i + 1 + l // (4 * QB)))
                if not (first and l < 2):
                    pe.wait_ge(max_done[0], s - 1)
                scores_a(l % 2, (ul // B) % 2, ul % B, qb, sa_done[0])

            def pair1(i, first=False, last=False):
                for l in range(4 * QB):
                    ul, qb = l // QB, l % QB
                    pe.wait_ge(shift_sem[SHIFT_BY[qb]], shift_count(i, l))
                    for j in range(2):
                        if not (first and l == 0):
                            pe.wait_ge(exp_done[0], 8 * QB * i + 2 * l + j - 1)
                        for k in range(4):
                            ins = nc.tensor.transpose(SB[j][:, k * P:(k + 1) * P],
                                                      logit[:, l % NT, (4 * j + k) * P:(4 * j + k + 1) * P], ident[:])
                        ins.then_inc(sb_done[0], 1)
                    if not (last and l + 3 >= 4 * QB):
                        block_a(i, l + 3, first)
                    if not (first and ul == 0):
                        if qb == 0:
                            before_av(0, i, ul - 1, not (first and ul < 3))
                            pe.wait_ge(exp_done[0], 2 * QB * (4 * i + ul))
                        weigh_v(0, (ul - 1) % 4, qb, qb == QB - 1)

            for l in range(3):
                block_a(0, l, True)
            pair1(0, first=True)
            with pe.Fori(1, PAIRS - 1) as i:
                pair1(i)
            pair1(PAIRS - 1, last=True)
            before_av(0, PAIRS - 1, 3, True)
            pe.wait_ge(exp_done[0], 2 * QB * U)
            for kb in range(QB):
                weigh_v(0, 3, kb, kb == QB - 1)

            def spread(a):
                for g in range(G):
                    pe.wait_ge(recip_done[a], g + 1)
                    nc.tensor.matmul(bank[:, g, :], head_sel[:], sums[:, g * N:(g + 1) * N], start=True, stop=True).then_inc(spread_mm[a], 1)

            spread(0)
            pe.wait_ge(o_ready[0], U)
            for g in range(G):
                pe.wait_ge(heads_scaled[0], g + 1)
                for tt in range(TG):
                    t = g * TG + tt
                    ins = nc.tensor.transpose(bank[:, 4 + g, tt * P:(tt + 1) * P], feat[:, t * P:(t + 1) * P], ident[:])
                ins.then_inc(nat_mm[0], 1)
            pe.wait_ge(nat_ready[0], G)
            transposes(1, 3)
            projections(1, w_qkv_sb[:, 0, :], w_qkv_sb[:, 1, :], w_qkv_sb[:, 2, :])

            pe.wait_ge(feat_ready[1], G)
            pe.wait_ge(part_rest[1], 2 * G)
            pe.wait_ge(v_evac[1], G)

            def block_a2(lu, qb, use, guard, loads=None):
                if loads is not None:
                    pe.wait_ge(qk_loaded[1][(lu // B) % 2], 16 * QK_DMAS * loads)
                if guard:
                    pe.wait_ge(max_done[1], use - 1)
                parity = (qb if lu == 0 else use_of_block(lu, qb)) % 2
                scores_a(parity, (lu // B) % 2, lu % B, qb, sa_done[1])

            def maxima_t(u, use, parity, slot):
                pe.wait_ge(split_step, 4 * u + 4)
                pe.wait_ge(max_done[1], use - 1)
                nc.tensor.transpose(SA[parity][0:3 * QB, 0, 0:P // 2].bitcast(bf16), max_parts[:, slot, :],
                                    ident_b[:]).then_inc(sa_done[1], 1)

            for qb in range(QB):
                block_a2(0, qb, qb, qb >= 2, 1 if qb == 0 else None)
            for qb in range(QB):
                block_a2(1, qb, use_of_block(1, qb), True)
                if qb == 2:
                    maxima_t(0, use_of_maxima(0), use_of_maxima(0) % 2, 0)

            def pair2(i, first=False, last=False):
                for ul in range(4):
                    u, lu = 4 * i + ul, ul + AU
                    head_slot, b = ul // B, ul % B
                    done = last and ul >= 2
                    if b == 0:
                        pe.wait_ge(qkb_loaded[head_slot], 16 * QK_DMAS * (i + 1))
                    pe.wait_ge(mrow_loaded[ul % 2], 16 * (2 * i + ul // 2 + 1))
                    for kb in range(QB):
                        lhs = kb_rows[:, head_slot, b * L + kb * P:b * L + (kb + 1) * P]
                        for half in range(2):
                            if not (first and ul == 0 and kb == 0):
                                pe.wait_ge(exp_done[1], 8 * QB * i + 2 * (QB * ul + kb) + half - 1)
                            nc.tensor.matmul(SB[half], lhs, qb_rows[:, head_slot, b * L + half * N:b * L + (half + 1) * N],
                                             start=True, stop=True).then_inc(sb_done[1], 1)
                        if not done:
                            block_a2(lu, kb, use_of_block(u + AU, kb), True,
                                     i + 1 + lu // 4 if kb == 0 and lu % 2 == 0 else None)
                        if kb == 2 and not (last and ul == 3):
                            maxima_t(u + 1, LAST_MAXIMA if done else use_of_maxima(u + 1),
                                     (LAST_MAXIMA if done else use_of_maxima(lu - 1)) % 2, (ul + 1) % 2)
                        if kb < 2:
                            if not (first and ul == 0):
                                pe.wait_ge(exp_done[1], 2 * (8 * (4 * i + ul - 1) + kb + 6) + 2)
                                weigh_v(1, (ul - 1) % 4, kb + 6, kb == 1)
                        else:
                            if kb == 2:
                                before_av(1, i, ul, not (first and ul < 2))
                            pe.wait_ge(exp_done[1], 2 * (8 * (4 * i + ul) + kb - 2) + 2)
                            weigh_v(1, ul, kb - 2, False)

            pair2(0, first=True)
            with pe.Fori(1, PAIRS - 1) as i:
                pair2(i)
            pair2(PAIRS - 1, last=True)
            pe.wait_ge(exp_done[1], 2 * QB * U)
            for kb in (6, 7):
                weigh_v(1, 3, kb, kb == 7)

            spread(1)
            pe.wait_ge(o_ready[1], U)
            for g in range(G):
                pe.wait_ge(heads_scaled[1], g + 1)
                for tt in range(TG):
                    t = g * TG + tt
                    ins = nc.tensor.matmul(bank[:, 4 + g, tt * P:(tt + 1) * P], feat[:, t * P:(t + 1) * P], w_proj_sb[:],
                                           start=True, stop=True)
                ins.then_inc(nat_mm[1], 1)

            pe.wait_ge(nat_ready[1], G)
            transposes(2, 4, token_rows[:, :, 0:D])
            for t in range(TT):
                pe.wait_ge(feat_ready[2], t // TG + 1)
                ins = nc.tensor.matmul(bank[:, 7, t * E:(t + 1) * E], feat[:, t * P:(t + 1) * P], gate_w_sb[:], start=True, stop=True)
            ins.then_inc(gate_mm, 1)
            pe.wait_ge(gate_step, 6)
            out_tiles_e = bank[:, 6, 0:(TT + 1) * E]
            nc.tensor.matmul(out_tiles_e, before[:], onehot[:].rearrange("p t e -> p (t e)"), start=True, stop=False)
            for t in range(TT):
                ins = nc.tensor.matmul(out_tiles_e[:, (t + 1) * E:], ones_b[:], spread_ap(onehot[:, t, :], [0, TT - t], [1, E]),
                                       start=False, stop=(t == TT - 1))
            ins.then_inc(rank_mm, 1)
            pe.wait_ge(feat_ready[2], G)
            for q in range(NS // 4):
                pe.wait_ge(slots_loaded[q], 16)
                if q >= 2:
                    pe.wait_ge(slot_t_ready, q - 1)
                for n in range(4):
                    ins = nc.tensor.transpose(bank[:, q % 2, n * P:(n + 1) * P], slot_rows[:, 4 * q + n, 0:D], ident[:])
                ins.then_inc(slot_t_mm, 1)

            def up(i, n, first):
                j = 4 * i + n
                pe.wait_ge(w_ready, j + 1)
                if not (first and n < 2):
                    pe.wait_ge(gelu_done, j - 1)
                for c in range(HC):
                    ins = nc.tensor.matmul(bank[:, 2 + n % 2, c * P:(c + 1) * P], w_ring[:, n, c * P:(c + 1) * P],
                                           slot_feat[:, bass.ds(j * P, P)], start=True, stop=True)
                ins.then_inc(up_mm, 1)

            def down(i, n, first):
                j = 4 * i + n
                pe.wait_ge(gelu_done, j + 1)
                if not first:
                    pe.wait_ge(y_ready, j - 1)
                for c in range(HC):
                    ins = nc.tensor.matmul(bank[:, 4 + n % 2, 0:D], hidden[:, n % 2, c, :],
                                           w_ring[:, n, HID + c * D:HID + (c + 1) * D], start=(c == 0), stop=(c == HC - 1))
                ins.then_inc(down_mm, 1)

            def four_tiles(i, first=False):
                for n in range(4):
                    up(i, n, first)
                    if n:
                        down(i, n - 1, first and n < 3)
                    elif not first:
                        down(i - 1, 3, False)

            pe.wait_ge(slot_t_ready, NS // 4)
            four_tiles(0, first=True)
            with pe.Fori(1, NS // 4) as i:
                four_tiles(i)
            down(NS // 4 - 1, 3, False)


_INS = ['L0_attn_x', 'L0_attn_w_in', 'L0_attn_kernel_offsets', 'L0_attn_kernel_amplitudes', 'L0_attn_kernel_sharpness',
        'L0_ffn_ln1_w', 'L0_ffn_ln1_b', 'L0_ffn_w_qkv', 'L0_ffn_w_proj', 'L0_ffn_ln2_w', 'L0_ffn_ln2_b',
        'L0_ffn_gate_w', 'L0_ffn_gate_b', 'L0_ffn_w1', 'L0_ffn_w2']


def kernel(**inputs):
    import numpy as _np
    import concourse.bacc as _bacc
    from concourse import mybir as _mybir
    from concourse.bass_utils import run_bass_kernel_spmd as _run

    nc = _bacc.Bacc("TRN2", target_bir_lowering=False, num_devices=1)
    arrays, args = {}, []
    for name in _INS:
        a = _np.ascontiguousarray(inputs[name])
        arrays[f"in_{name}_dram"] = a
        args.append(nc.dram_tensor(f"in_{name}_dram", a.shape, _mybir.dt.from_np(a.dtype), kind="ExternalInput").ap())
    shape = inputs['L0_attn_x'].shape
    args.append(nc.dram_tensor("out_dram", shape, _mybir.dt.float32, kind="ExternalOutput").ap())
    sandwich_kernel(nc, *args)
    r = _run(nc, [arrays], core_ids=[0])
    return r.results[0]["out_dram"]
```

```python
import concourse.bass as bass
from concourse import mybir
from contextlib import ExitStack
import numpy as np


def sandwich_kernel(nc, x, w_in, offsets, amplitudes, sharpness, ln1_w, ln1_b, w_qkv, w_proj,
                    ln2_w, ln2_b, gate_w, gate_b, w1, w2, out):
    fp32, bf16 = mybir.dt.float32, mybir.dt.bfloat16
    ALU, ACT, AX = mybir.AluOpType, mybir.ActivationFunctionType, mybir.AxisListType

    B, L, D = x.shape
    P = 128
    T = B * L
    TT = T // P
    H = offsets.shape[0]
    NK = offsets.shape[1]
    DH = D // H
    SCALE = float(np.float32(1.0) / np.sqrt(np.float32(DH)))
    EPS = 1e-5
    E, _, HID = w1.shape
    HC = HID // P
    U = B * H
    QB = L // P
    N = 512
    G = T // N
    TG = N // P
    LEAST = -3.0e38
    PAIRS = H // 2
    RUNS = [(0, 3, 0), (3, 2, 1), (5, 1, 2)]
    KR = 6 * DH
    QK_DMAS = 2 * len(RUNS)
    TAW = 2 * L - P
    VM = 32

    NS = (T - E) // P + E
    BODIES = -(-NS // 4)
    LAST = NS - 4 * (BODIES - 1)
    tokens_dram = nc.dram_tensor("tokens", (T, D), fp32, kind="Internal").ap()
    moe_dram = nc.dram_tensor("moe_out", (T + NS * P, D), fp32, kind="Internal").ap()
    parts_dram = [nc.dram_tensor(f"parts{a}", (2, 3, D, T), bf16, kind="Internal").ap() for a in range(2)]
    maxima_dram = nc.dram_tensor("maxima_rows", (2, 3 * QB, P), bf16, kind="Internal").ap()
    bias_dram = nc.dram_tensor("bias_rows", (H, 2 * L), fp32, kind="Internal").ap()

    with ExitStack() as ctx:
        def sb(name, shape, dt=fp32):
            return ctx.enter_context(nc.sbuf_tensor(name, shape, dt))

        def sem(name):
            return ctx.enter_context(nc.semaphore(name))

        x_res = sb("x_res", [P, TT, D])
        y_res = sb("y_res", [P, TT, D])
        norm = sb("norm", [P, TT, D])
        feat = sb("feat", [P, T])
        v_nat = sb("v_nat", [P, TT, D])
        q_rows = sb("q_rows", [P, 2, T], bf16)
        k_rows = sb("k_rows", [P, 2, T], bf16)
        tables = sb("tables", [P, 4096])
        bias_tab = tables[:, 0:2 * TAW].rearrange("p (s c) -> p s c", s=2)
        qb_rows = tables[:, 0:T].bitcast(bf16).rearrange("p (s n) -> p s n", s=2)
        kb_rows = tables[:, T:2 * T].bitcast(bf16).rearrange("p (s n) -> p s n", s=2)
        NT = 4
        logit = sb("logit", [P, NT, L])
        prob_mem = sb("prob_mem", [P, 2 * QB * L])
        prob = prob_mem[:, :].rearrange("p (s k q) -> p s k q", s=2, k=QB)
        bias_e = prob_mem[:, 0:4096].rearrange("p (t n) -> p t n", t=2)
        rel_pos = prob_mem[:, 4096:6144]
        bias_row = prob_mem[:, 6144:6144 + N]
        parts = prob_mem[:, 8192:14336].bitcast(bf16).rearrange("p (s t n) -> p s t n", s=2, t=3)
        rest = prob_mem[:, 14336:16384].rearrange("p (r s n) -> p r s n", r=2, s=2)
        WE = 2 * HID
        at = [0]

        def inside(n):
            at[0] += n
            return prob_mem[:, at[0] - n:at[0]]

        slot_rows = inside(4 * D).rearrange("p (r d) -> p r d", r=4)
        slot_feat = inside(4 * P).rearrange("p (r n) -> p r n", r=4)
        hidden = inside(2 * HID).rearrange("p (r c n) -> p r c n", r=2, c=HC)
        w_ring = inside(4 * WE).rearrange("p (r w) -> p r w", r=4)
        slot_y = inside(NS * D).rearrange("p (j d) -> p j d", j=NS)
        has_place = inside(TT * P // 2).bitcast(bf16).rearrange("p (t n) -> p t n", t=TT)
        assert at[0] <= 2 * QB * L
        v_ring = sb("v_ring", [P, 2, TT, VM])
        o_ring = sb("o_ring", [P, 2, L // 4])
        w_in_nat = sb("w_in_nat", [P, 3, D])
        w_in_t = sb("w_in_t", [P, 3, D])
        w_qkv_sb = sb("w_qkv_sb", [P, 3, D])
        w_proj_sb = sb("w_proj_sb", [P, D])
        gate_w_sb = sb("gate_w_sb", [P, E])
        gate_b_sb = sb("gate_b_sb", [P, E])
        w_moe = sb("w_moe", [P, E, 2 * HID])
        ln_par = sb("ln_par", [P, 4])
        bias_par = sb("bias_par", [P, 3, 2])
        neg_sharp = sb("neg_sharp", [P, 2])
        amp_sel = sb("amp_sel", [P, 2, VM])
        ident = sb("ident", [P, P])
        ident_b = sb("ident_b", [P, P], bf16)
        eps_col = sb("eps_col", [P, 1])
        order = sb("order", [P, E])
        stats = sb("stats", [P, TT, 6])
        meanvar = sb("meanvar", [P, TT, 2])
        std = sb("std", [P, TT])
        rstd = sb("rstd", [P, TT])
        shift_by = sb("shift_by", [P, TT])
        recip = sb("recip", [P, 2, 4, 2])
        row_max = sb("row_max", [P, QB])
        unit_max = sb("unit_max", [P, 2, QB])
        max_rest = sb("max_rest", [P, 2, QB])
        max_parts = sb("max_parts", [P, 2, 3 * QB], bf16)
        max_rows = sb("max_rows", [3 * QB, 2, P], bf16)
        gate = sb("gate", [P, TT, E])
        gate_max = sb("gate_max", [P, TT, 1])
        onehot = sb("onehot", [P, TT + 1, E], bf16)
        before = sb("before", [P, P], bf16)
        ones_b = sb("ones_b", [P, P], bf16)
        lower = sb("lower", [P, E, E])
        tile_start = sb("tile_start", [P, NS + 1])
        tile_no = sb("tile_no", [P, NS])
        next_tile_no = sb("next_tile_no", [P, TT])
        row_no = sb("row_no", [P, 1])
        col_no = sb("col_no", [P, P])
        spare_no = sb("spare_no", [P, NS])
        counts = sb("counts", [P, E, TT])
        tiles_of = sb("tiles_of", [P, E, 1])
        pairs_ef = sb("pairs_ef", [P, E, E])
        first_tile = sb("first_tile", [P, E, 1])
        end_tile = sb("end_tile", [P, E, 1])
        place = sb("place", [P, TT, E])
        slot_f = sb("slot_f", [P, TT])
        at_least = sb("at_least", [P, TT, NS + 1])
        in_tile = sb("in_tile", [P, TT, NS])
        slot_tile = sb("slot_tile", [P, TT])
        place_in_tile = sb("place_in_tile", [P, TT])
        numbers = sb("numbers", [P, TT, 2, NS], bf16)
        slot_token = sb("slot_token", [P, NS])
        unused = sb("unused", [P, NS])
        gather_u = sb("gather_u", [P, NS], mybir.dt.uint32)
        ended = sb("ended", [P, NS, E])
        expert_f = sb("expert_f", [P, NS])
        expert_u = sb("expert_u", [P, NS], mybir.dt.uint32)
        token_u = sb("token_u", [P, NS], mybir.dt.uint32)

        bank = ctx.enter_context(nc.psum_tensor("bank", [P, 8, N], fp32))
        SA = [bank[:, 0:2, :], bank[:, 2:4, :]]
        SB = [bank[:, 4, :], bank[:, 5, :]]
        AV = [bank[:, 6, :], bank[:, 7, :]]

        def spread_ap(ap, *dims):
            return bass.AP(ap.tensor, ap.offset, [list(ap.ap[0])] + [list(d) for d in dims])

        x_loaded = [sem(f"x_loaded{g}") for g in range(G)]
        bias_loaded = sem("bias_loaded")
        w_in_loaded = sem("w_in_loaded")
        weights_loaded = sem("weights_loaded")
        moe_loaded = sem("moe_loaded")
        consts_ready = sem("consts_ready")
        pool_step = sem("pool_step")
        ident_ready = sem("ident_ready")
        mask_ready = sem("mask_ready")
        ones_ready = sem("ones_ready")
        sharp_ready = sem("sharp_ready")
        amp_ready = sem("amp_ready")
        bias_sq = sem("bias_sq")
        bias_exp = sem("bias_exp")
        bias_mm = sem("bias_mm")
        bias_out = sem("bias_out")
        bias_stored = sem("bias_stored")
        w_t_mm = sem("w_t_mm")
        w_t_ready = sem("w_t_ready")
        ln_stats = sem("ln_stats")
        ln_aggr = sem("ln_aggr")
        ln_std = sem("ln_std")
        ln_rstd = sem("ln_rstd")
        ln_shift = sem("ln_shift")
        ln_out_dve = sem("ln_out_dve")
        ln_out_act = sem("ln_out_act")
        tp_done = sem("tp_done")
        feat_ready = sem("feat_ready")
        gate_feat_ready = sem("gate_feat_ready")
        q_mm = [sem(f"q{a}_mm") for a in range(2)]
        k_mm = [sem(f"k{a}_mm") for a in range(2)]
        v_mm = [sem(f"v{a}_mm") for a in range(2)]
        part_hi = [sem(f"part{a}_hi") for a in range(2)]
        part_rest = [sem(f"part{a}_rest") for a in range(2)]
        part_mid = [sem(f"part{a}_mid") for a in range(2)]
        part_lo = [sem(f"part{a}_lo") for a in range(2)]
        v_evac = [sem(f"v{a}_evac") for a in range(2)]
        parts_stored = [sem(f"parts{a}_stored") for a in range(2)]
        first_loaded = [sem(f"first{a}_loaded") for a in range(2)]
        qk_loaded = [[sem(f"qk{a}_loaded{s}") for s in range(2)] for a in range(2)]
        qkb_loaded = [sem(f"qkb_loaded{s}") for s in range(2)]
        kb_minus = sem("kb_minus")
        tab_loaded = [sem(f"tab_loaded{s}") for s in range(2)]
        sa_done = [sem(f"sa{a}_done") for a in range(2)]
        max_done = [sem(f"max{a}_done") for a in range(2)]
        shift_dve = sem("shift_dve")
        shift_act = sem("shift_act")
        sb_done = [sem(f"sb{a}_done") for a in range(2)]
        exp_done = [sem(f"exp{a}_done") for a in range(2)]
        v_ready = [sem(f"v{a}_ready") for a in range(2)]
        av_done = [sem(f"av{a}_done") for a in range(2)]
        o_ready = [sem(f"o{a}_ready") for a in range(2)]
        unit_t_mm = [sem(f"unit{a}_t_mm") for a in range(2)]
        unit_recip = [sem(f"unit{a}_recip") for a in range(2)]
        unit_scaled = [sem(f"unit{a}_scaled") for a in range(2)]
        split_step = sem("split_step")
        max_t_mm = sem("max_t_mm")
        max_copied = sem("max_copied")
        mrow_stored = sem("mrow_stored")
        mrow_loaded = [sem(f"mrow_loaded{s}") for s in range(2)]
        proj_mm = sem("proj_mm")
        proj_added = sem("proj_added")
        x_added = [sem(f"x_added_{e}") for e in ("dve", "pool")]
        gate_mm = sem("gate_mm")
        gate_step = sem("gate_step")
        moe_consts_ready = sem("moe_consts_ready")
        tokens_stored = sem("tokens_stored")
        rank_mm = sem("rank_mm")
        numbers_ready = sem("numbers_ready")
        numbers_mm = sem("numbers_mm")
        gather_known = sem("gather_known")
        expert_known = sem("expert_known")
        slots_loaded = [sem(f"slots_loaded{n}") for n in range(4)]
        slot_t_mm = sem("slot_t_mm")
        slot_t_ready = sem("slot_t_ready")
        tokens_known = sem("tokens_known")
        w_ready = sem("w_ready")
        up_mm = sem("up_mm")
        gelu_done = sem("gelu_done")
        down_mm = sem("down_mm")
        y_ready = sem("y_ready")
        y_scattered = sem("y_scattered")
        y_loaded = [sem(f"y_loaded{g}") for g in range(G)]
        y_added = [sem(f"y_added_{e}") for e in ("dve", "pool")]
        out_ready = sem("out_ready")
        out_stored = sem("out_stored")
        past_wait_dve = sem("past_wait_dve")
        past_wait_pool = sem("past_wait_pool")

        SHIFT_BY = "ADADADAD"
        shift_sem = {"D": shift_dve, "A": shift_act}

        def shift_count(i, l):
            who = SHIFT_BY[l % QB]
            per_body = 4 * SHIFT_BY.count(who)
            return i * per_body + sum(SHIFT_BY[m % QB] == who for m in range(l + 1))

        ACT_TILES = (1, 2, 2, 1, 1, 2)

        def act_tiles_before(n):
            return G * sum(ACT_TILES[:n])

        def dve_tiles_before(n):
            return n * TT - act_tiles_before(n)

        def norm_group_out(eng, n, g):
            eng.wait_ge(ln_out_dve, dve_tiles_before(n) + (g + 1) * (TG - ACT_TILES[n]))
            eng.wait_ge(ln_out_act, act_tiles_before(n) + (g + 1) * ACT_TILES[n])

        WARM = 12
        MAX_AT = 2
        max_t = [bank[0:3 * QB, 6 + n, L // 4:L // 4 + P // 2].bitcast(bf16) for n in range(2)]
        AU = 2

        ctx.enter_context(nc.allow_non_contiguous_dma(reason="head rows and skewed tables"))
        block = ctx.enter_context(nc.Block())

        @block.sync
        def _(sp):
            x_tiles = x.rearrange("b (t p) d -> p (b t) d", p=P)
            for g in range(G):
                sp.dma_start(x_res[:, g * TG:(g + 1) * TG, :], x_tiles[:, g * TG:(g + 1) * TG, :]).then_inc(x_loaded[g], 16)
                if g == 0:
                    for n, v in enumerate((offsets, amplitudes, sharpness)):
                        sp.dma_start(bias_par[:, n, :], v.rearrange("(t h) k -> (h k) t", t=2)).then_inc(bias_loaded, 16)
            sp.dma_start(w_in_nat[:], w_in.rearrange("(c p) d -> p c d", p=P)).then_inc(w_in_loaded, 16)
            sp.dma_start(w_qkv_sb[:], w_qkv.rearrange("d (c n) -> d c n", c=3)).then_inc(weights_loaded, 16)
            sp.dma_start(w_proj_sb[:], w_proj).then_inc(weights_loaded, 16)
            sp.dma_start(gate_w_sb[:], gate_w).then_inc(weights_loaded, 16)
            sp.dma_start(gate_b_sb[:], bass.AP(gate_b.tensor, gate_b.offset, [[0, P], [1, E]])).then_inc(weights_loaded, 16)
            for n, v in enumerate((ln1_w, ln1_b, ln2_w, ln2_b)):
                sp.dma_start(ln_par[:, n:n + 1], v.rearrange("(d o) -> d o", o=1)).then_inc(weights_loaded, 16)

            def store_bias():
                sp.wait_ge(bias_out, 1)
                for c in range(4):
                    sp.dma_start(bias_dram[:, c * N:(c + 1) * N], bias_row[VM * c:VM * c + H, :]).then_inc(bias_stored, 16)

            def store_parts(a, groups):
                for g in groups:
                    for s in range(2):
                        sp.wait_ge(part_lo[a], 2 * g + s + 1)
                        sp.dma_start(parts_dram[a][s, :, :, g * N:(g + 1) * N].rearrange("t p n -> p t n"),
                                     parts[:, s, :, g * N:(g + 1) * N]).then_inc(parts_stored[a], 16)
                    if a == 0 and g == 0:
                        store_bias()
                    if a == 0 and g == 1:
                        sp.wait_ge(bias_stored, 16 * 4)
                        table_of(0, 0)
                sp.wait_ge(parts_stored[a], 16 * 2 * (groups[-1] + 1))

            def rows_of(a, h, slot, q_dst, k_dst, loaded, tokens=slice(0, T)):
                for row, n, k_part in RUNS:
                    at = slice(row * DH, (row + n) * DH)
                    sp.dma_start(q_dst[at, slot, tokens],
                                 parts_dram[a][0, 0:n, bass.ds(h * DH, DH), tokens]).then_inc(loaded, 16)
                    k_src = parts_dram[a][1, k_part, bass.ds(h * DH, DH), tokens]
                    sp.dma_start(k_dst[at, slot, tokens],
                                 bass.AP(k_src.tensor, k_src.offset, [[0, n], [T, DH], [1, tokens.stop - tokens.start]])
                                 ).then_inc(loaded, 16)

            def first_rows(a):
                store_parts(a, range(G // 2))
                rows_of(a, 0, 0, q_rows, k_rows, first_loaded[a], slice(0, L))
                store_parts(a, range(G // 2, G))
                rows_of(a, 0, 0, q_rows, k_rows, qk_loaded[a][0], slice(L, T))

            def table_of(h, slot):
                row = bias_dram[bass.ds(h, 1), 0:TAW]
                src = bass.AP(row.tensor, row.offset, [[1, P], [1, TAW]])
                sp.dma_start(bias_tab[:, slot, :], src).then_inc(tab_loaded[slot], 16)

            sp.wait_ge(ones_ready, 1)
            first_rows(0)
            rows_of(0, 1, 1, q_rows, k_rows, qk_loaded[0][1])
            table_of(1, 1)
            sp.dma_start(w_moe[:, :, 0:HID], w1.rearrange("e d n -> d e n")).then_inc(moe_loaded, 16)
            for e in range(E):
                sp.dma_start(w_moe[:, e, HID:2 * HID].rearrange("p (c d) -> p c d", c=HC),
                             w2[e].rearrange("(c p) d -> p c d", p=P)).then_inc(moe_loaded, 16)

            def pair1(i):
                for hl in range(2):
                    h = 2 * i + hl
                    sp.wait_ge(sa_done[0], QB * B * (h + 1))
                    rows_of(0, h + 2, hl, q_rows, k_rows, qk_loaded[0][hl])
                    sp.wait_ge(max_done[0], QB * B * (h + 1))
                    table_of(h + 2, hl)

            pair1(0)
            with sp.Fori(1, PAIRS - 1) as i:
                pair1(i)

            first_rows(1)
            rows_of(1, 1, 1, q_rows, k_rows, qk_loaded[1][1])
            sp.wait_ge(kb_minus, 4)
            rows_of(1, 0, 0, qb_rows, kb_rows, qkb_loaded[0])

            def maxima_of(u, slot):
                sp.wait_ge(max_copied, u + 1)
                head_slot, b = (slot // B) % 2, slot % B
                sp.dma_start(maxima_dram[slot % 2], max_rows[:, slot % 2, :]).then_inc(mrow_stored, 16)
                sp.wait_ge(mrow_stored, 16 * (u + 1))
                sp.dma_start(qb_rows[KR:KR + 3, head_slot, b * L:(b + 1) * L],
                             maxima_dram[slot % 2].rearrange("(p q) c -> p (q c)", p=3)).then_inc(mrow_loaded[slot % 2], 16)

            maxima_of(0, 0)
            rows_of(1, 1, 1, qb_rows, kb_rows, qkb_loaded[1])

            def pair2(i, first=False, last=False):
                for ul in range(4):
                    u = 4 * i + ul
                    if not (last and ul == 3):
                        maxima_of(u + 1, (ul + 1) % 4)
                    if ul % 2 == 0:
                        hb = 2 * i + ul // 2 + 1
                        slot = (ul // 2 + 1) % 2
                        if not (first and ul == 0):
                            sp.wait_ge(sb_done[1], 2 * QB * u)
                            if not (last and ul == 2):
                                rows_of(1, hb, slot, qb_rows, kb_rows, qkb_loaded[slot])
                        if not last:
                            sp.wait_ge(sa_done[1], QB * (u + AU))
                            rows_of(1, hb + 1, 1 - slot, q_rows, k_rows, qk_loaded[1][1 - slot])

            pair2(0, first=True)
            with sp.Fori(1, PAIRS - 1) as i:
                pair2(i)
            pair2(PAIRS - 1, last=True)

            token_tiles = tokens_dram.rearrange("(t p) d -> p t d", p=P)
            for g in range(G):
                norm_group_out(sp, 4, g)
                sp.dma_start(token_tiles[:, g * TG:(g + 1) * TG, :], norm[:, g * TG:(g + 1) * TG, :]).then_inc(tokens_stored, 16)
            sp.wait_ge(y_scattered, 16 * NS)
            moe_tiles = moe_dram[0:T].rearrange("(t p) d -> p t d", p=P)
            for g in range(G):
                sp.dma_start(norm[:, g * TG:(g + 1) * TG, :], moe_tiles[:, g * TG:(g + 1) * TG, :]).then_inc(y_loaded[g], 16)

            out_tiles = out.rearrange("b (t p) d -> p (b t) d", p=P)
            for g in range(G):
                sp.wait_ge(out_ready, g + 1)
                sp.dma_start(out_tiles[:, g * TG:(g + 1) * TG, :], norm[:, g * TG:(g + 1) * TG, :]).then_inc(out_stored, 16)
            sp.wait_ge(out_stored, 16 * G)

        @block.gpsimd
        def _(pool):
            steps = [0]

            def chain(ins):
                steps[0] += 1
                ins.then_inc(pool_step, 1)
                pool.wait_ge(pool_step, steps[0])

            nc.gpsimd.iota(rel_pos, [[-1, 2 * L]], base=L - 1, channel_multiplier=0,
                           allow_small_or_imprecise_dtypes=True).then_inc(consts_ready, 1)
            chain(nc.gpsimd.memset(ident[:], 0.0))
            chain(nc.gpsimd.affine_select(out=ident[:], in_=ident[:], compare_op=ALU.not_equal, fill=1.0, base=0,
                                          pattern=[[-1, P]], channel_multiplier=1))
            nc.gpsimd.tensor_copy(ident_b[:], ident[:]).then_inc(ident_ready, 1)
            nc.gpsimd.memset(eps_col[:], EPS).then_inc(ident_ready, 1)
            chain(nc.gpsimd.memset(amp_sel[:], 1.0))
            chain(nc.gpsimd.affine_select(out=amp_sel[:], in_=amp_sel[:], compare_op=ALU.is_ge, fill=0.0, base=0,
                                          pattern=[[P, 2], [-NK, VM]], channel_multiplier=1))
            nc.gpsimd.affine_select(out=amp_sel[:], in_=amp_sel[:], compare_op=ALU.is_ge, fill=0.0,
                                    base=NK - 1, pattern=[[-P, 2], [NK, VM]], channel_multiplier=-1).then_inc(mask_ready, 1)
            pool.wait_ge(ident_ready, 2)
            pool.wait_ge(mask_ready, 1)
            for rows in (q_rows, k_rows):
                chain(nc.gpsimd.memset(rows[32:64], 0.0))
                chain(nc.gpsimd.memset(rows[64:P], 0.0))
            chain(nc.gpsimd.memset(v_ring[:], 0.0))
            chain(nc.gpsimd.memset(v_ring[:, :, :, DH:DH + 1], 1.0))
            pool.sem_inc(ones_ready, 1)
            nc.gpsimd.iota(order[:], [[-1, E]], base=E, channel_multiplier=0,
                           allow_small_or_imprecise_dtypes=True).then_inc(consts_ready, 1)
            pool.wait_ge(consts_ready, 2)
            chain(nc.gpsimd.memset(onehot[:], 0.0))
            chain(nc.gpsimd.memset(ones_b[:], 1.0))
            chain(nc.gpsimd.affine_select(out=before[:], in_=ones_b[:], compare_op=ALU.is_gt, fill=0.0, base=0,
                                          pattern=[[1, P]], channel_multiplier=-1))
            chain(nc.gpsimd.memset(lower[:], 1.0))
            chain(nc.gpsimd.affine_select(out=lower[:], in_=lower[:], compare_op=ALU.is_gt, fill=0.0, base=0,
                                          pattern=[[1, E], [-1, E]], channel_multiplier=0))
            for dst, pattern, base, per_row in ((tile_start, [[P, NS + 1]], 0, 0), (tile_no, [[1, NS]], 0, 0),
                                                (next_tile_no, [[1, TT]], 1, 0), (row_no, [[0, 1]], 0, 1),
                                                (col_no, [[1, P]], 0, 0), (spare_no, [[P, NS]], P + T, 1)):
                chain(nc.gpsimd.iota(dst[:], pattern, base=base, channel_multiplier=per_row,
                                     allow_small_or_imprecise_dtypes=True))
            pool.sem_inc(moe_consts_ready, 1)

            def v_of(a, h, slot, wait):
                if wait:
                    pool.wait_ge(av_done[a], B * (h - 1))
                pool.sem_inc(past_wait_pool, 1)
                nc.gpsimd.tensor_copy(v_ring[:, slot, :, 0:DH],
                                      v_nat[:, :, bass.ds(h * DH, DH)]).then_inc(v_ready[a], 1)

            pool.wait_ge(v_evac[0], G)

            def pair1(i, first=False):
                for hl in range(2):
                    v_of(0, 2 * i + hl, hl, not first)

            pair1(0, first=True)
            with pool.Fori(1, PAIRS) as i:
                pair1(i)

            pool.wait_ge(max_done[0], QB * U)
            pool.wait_ge(v_ready[0], H)
            nc.gpsimd.memset(kb_rows[32:64], -1.0).then_inc(kb_minus, 1)
            pool.wait_ge(kb_minus, 1)
            nc.gpsimd.memset(kb_rows[64:P], 0.0).then_inc(kb_minus, 1)
            nc.gpsimd.memset(qb_rows[64:P], 0.0).then_inc(kb_minus, 1)
            pool.wait_ge(kb_minus, 3)
            nc.gpsimd.memset(qb_rows[32:64], 0.0).then_inc(kb_minus, 1)
            pool.wait_ge(kb_minus, 4)

            def add_odd_groups(dst, wait, added):
                for g in range(1, G, 2):
                    ts = slice(g * TG, (g + 1) * TG)
                    wait(g)
                    nc.gpsimd.tensor_tensor(dst[:, ts, :], dst[:, ts, :], norm[:, ts, :], ALU.add).then_inc(added, 1)

            add_odd_groups(x_res, lambda g: norm_group_out(pool, 1, g), x_added[1])

            def split_maxima(u, slot):
                pool.wait_ge(max_done[1], QB * (u + 1))
                m, r = unit_max[:, slot, :], max_rest[:, slot]
                hi, mid, lo = (max_parts[:, slot, n * QB:(n + 1) * QB] for n in range(3))
                pool.sem_inc(past_wait_pool, 1)
                nc.gpsimd.tensor_copy(hi, m).then_inc(split_step, 1)
                pool.wait_ge(split_step, 4 * u + 1)
                nc.gpsimd.tensor_tensor(mid, m, hi, ALU.subtract).then_inc(split_step, 1)
                nc.gpsimd.tensor_tensor(r, m, hi, ALU.subtract).then_inc(split_step, 1)
                pool.wait_ge(split_step, 4 * u + 3)
                nc.gpsimd.tensor_tensor(lo, r, mid, ALU.subtract).then_inc(split_step, 1)

            pool.wait_ge(v_evac[1], G)
            pool.wait_ge(av_done[0], U)
            split_maxima(0, 0)
            split_maxima(1, 1)

            def pair2(i, first=False, last=False):
                for ul in range(4):
                    if ul % 2 == 0:
                        v_of(1, 2 * i + ul // 2, ul // 2, not first)
                    if not (last and ul >= 2):
                        split_maxima(4 * i + ul + AU, ul % 2)

            pair2(0, first=True)
            with pool.Fori(1, PAIRS - 1) as i:
                pair2(i)
            pair2(PAIRS - 1, last=True)

            pool.wait_ge(tokens_stored, 16 * G)

            def gather(j):
                if j >= 4:
                    pool.wait_ge(slot_t_mm, j - 3)
                nc.gpsimd.indirect_dma_start(out=slot_rows[:, j % 4, :], out_offset=None, in_=tokens_dram,
                                             in_offset=bass.IndirectOffsetOnAxis(ap=gather_u[:, j:j + 1], axis=0)
                                             ).then_inc(slots_loaded[j % 4], 16)

            AHEAD = 6
            pool.wait_ge(gather_known, 1)
            for j in range(AHEAD):
                gather(j)
            pool.wait_ge(tokens_known, 1)
            for j in range(NS):
                pool.wait_ge(y_ready, j + 1)
                nc.gpsimd.indirect_dma_start(out=moe_dram, out_offset=bass.IndirectOffsetOnAxis(ap=token_u[:, j:j + 1], axis=0),
                                             in_=slot_y[:, j, :], in_offset=None).then_inc(y_scattered, 16)
                if j + AHEAD < NS:
                    gather(j + AHEAD)
            add_odd_groups(y_res, lambda g: pool.wait_ge(y_loaded[g], 16), y_added[1])

        @block.scalar
        def _(act):
            def norm_part(n, src, dst):
                act.wait_ge(ln_aggr, (n + 1) * TT)
                nc.scalar.activation(std[:], meanvar[:, :, 1], ACT.Sqrt, bias=eps_col[:, 0:1]).then_inc(ln_std, 1)
                act.wait_ge(ln_shift, n + 1)
                for g in range(G):
                    for t in range((g + 1) * TG - ACT_TILES[n], (g + 1) * TG):
                        nc.scalar.activation(dst[:, t, :], src[:, t, :], ACT.Identity, scale=rstd[:, t:t + 1],
                                             bias=shift_by[:, t:t + 1]).then_inc(ln_out_act, 1)

            def projections(a):
                for g in range(G):
                    cols = slice(g * N, (g + 1) * N)
                    act.wait_ge(q_mm[a], g + 1)
                    nc.scalar.activation(parts[:, 0, 0, cols], bank[:, 4 + 2 * (g % 2), :], ACT.Copy,
                                         scale=SCALE).then_inc(part_hi[a], 1)
                    act.wait_ge(k_mm[a], g + 1)
                    nc.scalar.copy(parts[:, 1, 0, cols], bank[:, 5 + 2 * (g % 2), :]).then_inc(part_hi[a], 1)
                    act.wait_ge(v_mm[a], g + 1)
                    nc.scalar.copy(v_nat[:, g * TG:(g + 1) * TG, :],
                                   bank[:, g, :].rearrange("p (t d) -> p t d", t=TG)).then_inc(v_evac[a], 1)
                    for s in range(2):
                        act.wait_ge(part_rest[a], 2 * g + s + 1)
                        nc.scalar.copy(parts[:, s, 1, cols], rest[:, g % 2, s, :]).then_inc(part_mid[a], 1)

            act.wait_ge(consts_ready, 1)
            act.wait_ge(bias_loaded, 48)
            for t in range(2):
                nc.scalar.activation(bias_e[:, t, :], rel_pos, ACT.Square, bias=bias_par[:, 0, t:t + 1]).then_inc(bias_sq, 1)
            act.wait_ge(ident_ready, 2)
            norm_part(0, x_res, norm)
            act.wait_ge(w_t_mm, 1)
            nc.scalar.copy(w_in_t[:].rearrange("p c d -> p (c d)"), bank[:, 4, 0:3 * D]).then_inc(w_t_ready, 1)
            act.wait_ge(sharp_ready, 2)
            for t in range(2):
                act.wait_ge(bias_sq, t + 1)
                nc.scalar.activation(bias_e[:, t, :], bias_e[:, t, :], ACT.Exp,
                                     scale=neg_sharp[:, t:t + 1]).then_inc(bias_exp, 1)

            def evacuate(a, u, slot, wait):
                act.wait_ge(av_done[a], u + 1)
                if wait:
                    act.wait_ge(unit_t_mm[a], u - 1)
                nc.scalar.copy(o_ring[:, slot, :], AV[slot][:, 0:L // 4]).then_inc(o_ready[a], 1)

            projections(0)

            def shift(i, l):
                if SHIFT_BY[l % QB] == "A":
                    act.wait_ge(max_done[0], 4 * QB * i + l + 1)
                    t = logit[:, l % NT, :]
                    nc.scalar.activation(t, t, ACT.Identity, scale=-1.0,
                                         bias=row_max[:, l % QB:l % QB + 1]).then_inc(shift_act, 1)

            def pair1(i, first=False, last=False):
                for l in range(4 * QB):
                    ul, qb = l // QB, l % QB
                    if qb == 1 and not (first and ul < 2):
                        evacuate(0, 4 * i + ul - 2, ul % 2, not (first and ul < 4))
                    if qb == 0 and not (first and ul < 2):
                        act.wait_ge(av_done[0], 4 * i + ul - 1)
                    for j in range(2):
                        act.wait_ge(sb_done[0], 8 * QB * i + 2 * l + j + 1)
                        nc.scalar.activation(prob[:, ul % 2, 4 * j:4 * j + 4, qb * P:(qb + 1) * P],
                                             SB[j].rearrange("p (k q) -> p k q", k=4), ACT.Exp,
                                             scale=-1.0 if SHIFT_BY[qb] == "A" else 1.0).then_inc(exp_done[0], 1)
                    if not (last and l + 2 >= 4 * QB):
                        shift(i, l + 2)

            for l in range(2):
                shift(0, l)
            pair1(0, first=True)
            with act.Fori(1, PAIRS - 1) as i:
                pair1(i)
            pair1(PAIRS - 1, last=True)
            for u in (U - 2, U - 1):
                evacuate(0, u, u % 2, True)

            norm_part(1, norm, norm)
            norm_part(2, x_res, y_res)
            norm_part(3, y_res, norm)
            projections(1)

            def pair2(i, first=False, last=False):
                for ul in range(4):
                    u = 4 * i + ul
                    if not (first and ul < 2):
                        act.wait_ge(av_done[1], u - 1)
                    for kb in range(QB):
                        if kb == 2 and not (first and ul < 1):
                            evacuate(1, u - 1, (ul - 1) % 2, not (first and ul < 3))
                        for half in range(2):
                            act.wait_ge(sb_done[1], 8 * QB * i + 2 * (QB * ul + kb) + half + 1)
                            nc.scalar.activation(prob[:, ul % 2, kb, half * N:(half + 1) * N], SB[half],
                                                 ACT.Exp).then_inc(exp_done[1], 1)

            pair2(0, first=True)
            with act.Fori(1, PAIRS) as i:
                pair2(i)
            evacuate(1, U - 1, (U - 1) % 2, True)

            norm_part(4, y_res, norm)
            for g in range(G // 2):
                act.wait_ge(tp_done, 3 * G + g + 1)
                nc.scalar.activation(feat[:, g * N:(g + 1) * N], bank[:, g, :], ACT.Identity, scale=ln_par[:, 2:3],
                                     bias=ln_par[:, 3:4]).then_inc(feat_ready, 1)

            def four_tiles(i, first=False, tiles=4):
                for n in range(tiles):
                    j = 4 * i + n
                    act.wait_ge(up_mm, j + 1)
                    if not (first and n < 2):
                        act.wait_ge(down_mm, j - 1)
                    nc.scalar.activation(hidden[:, n % 2, :, :], bank[:, 2 + n % 2, :].rearrange("p (c n) -> p c n", c=HC),
                                         ACT.Gelu_apprx_tanh).then_inc(gelu_done, 1)

            four_tiles(0, first=True)
            with act.Fori(1, BODIES - 1) as i:
                four_tiles(i)
            four_tiles(BODIES - 1, tiles=LAST)
            norm_part(5, y_res, norm)

        @block.vector
        def _(dve):
            dve.wait_ge(bias_loaded, 48)
            nc.vector.tensor_scalar(neg_sharp[:], bias_par[:, 2, :], -1.0, None, ALU.mult).then_inc(sharp_ready, 1)
            dve.wait_ge(sharp_ready, 1)
            nc.vector.tensor_tensor(neg_sharp[:], neg_sharp[:], bias_par[:, 2, :], ALU.min).then_inc(sharp_ready, 1)

            def norm_stats(n, src, before=None):
                for t in range(TT):
                    if before and t % TG == 0:
                        before(t // TG)
                    nc.vector.bn_stats(stats[:, t, :], src[:, t, :]).then_inc(ln_stats, 1)
                for t in range(TT):
                    dve.wait_ge(ln_stats, n * TT + t + 1)
                    nc.vector.bn_aggr(meanvar[:, t, :], stats[:, t, :]).then_inc(ln_aggr, 1)

            def norm_apply(n, src, dst, then=None, then_groups=range(G)):
                dve.wait_ge(ln_std, n + 1)
                nc.vector.reciprocal(rstd[:], std[:]).then_inc(ln_rstd, 1)
                dve.wait_ge(ln_rstd, n + 1)
                nc.vector.scalar_tensor_tensor(shift_by[:], meanvar[:, :, 0], -1.0, rstd[:], ALU.mult,
                                               ALU.mult).then_inc(ln_shift, 1)
                for g in range(G):
                    for t in range(g * TG, (g + 1) * TG - ACT_TILES[n]):
                        nc.vector.tensor_scalar(dst[:, t, :], src[:, t, :], meanvar[:, t, 0:1], rstd[:, t:t + 1],
                                                ALU.subtract, ALU.mult).then_inc(ln_out_dve, 1)
                if then:
                    for g in then_groups:
                        norm_group_out(dve, n, g)
                        then(g, slice(g * TG, (g + 1) * TG))

            norm_stats(0, x_res, lambda g: dve.wait_ge(x_loaded[g], 16))
            norm_apply(0, x_res, norm)
            dve.wait_ge(mask_ready, 1)
            for t in range(2):
                ins = nc.vector.tensor_scalar(amp_sel[:, t, :], amp_sel[:, t, :], bias_par[:, 1, t:t + 1], None, ALU.mult)
            ins.then_inc(amp_ready, 1)

            def feature_major(a, par=None, groups=range(G), banks=G, ready=feat_ready):
                for g in groups:
                    dve.wait_ge(tp_done, a * G + g + 1)
                    dst, src = feat[:, g * N:(g + 1) * N], bank[:, g % banks, :]
                    if par is None:
                        nc.vector.tensor_copy(dst, src).then_inc(ready, 1)
                    else:
                        nc.vector.tensor_scalar(dst, src, ln_par[:, par:par + 1], ln_par[:, par + 1:par + 2],
                                                ALU.mult, ALU.add).then_inc(ready, 1)

            def projections(a):
                for g in range(G):
                    cols = slice(g * N, (g + 1) * N)
                    for s in range(2):
                        dve.wait_ge(part_hi[a], 2 * g + s + 1)
                        if g >= 2:
                            dve.wait_ge(part_lo[a], 2 * (g - 2) + s + 1)
                        nc.vector.scalar_tensor_tensor(rest[:, g % 2, s, :], bank[:, 4 + 2 * (g % 2) + s, :], SCALE if s == 0 else 1.0,
                                                       parts[:, s, 0, cols], ALU.mult, ALU.subtract).then_inc(part_rest[a], 1)
                    for s in range(2):
                        dve.wait_ge(part_mid[a], 2 * g + s + 1)
                        nc.vector.tensor_tensor(parts[:, s, 2, cols], rest[:, g % 2, s, :], parts[:, s, 1, cols],
                                                ALU.subtract).then_inc(part_lo[a], 1)
                    if a == 0 and g == 0:
                        dve.wait_ge(bias_mm, 1)
                        nc.vector.tensor_copy(bias_row, bank[:, 3, :]).then_inc(bias_out, 1)

            feature_major(0)
            projections(0)

            def scale_unit(a, u, h, b, slot):
                out_t = AV[slot][:, L // 4:L // 2].rearrange("p (s c m) -> p c s m", s=2, c=4)
                dve.wait_ge(unit_t_mm[a], u + 1)
                dve.sem_inc(past_wait_dve, 1)
                nc.vector.reciprocal(recip[:, slot], out_t[:, :, :, DH]).then_inc(unit_recip[a], 1)
                dve.wait_ge(unit_recip[a], u + 1)
                dve.sem_inc(past_wait_dve, 1)
                nc.vector.tensor_tensor(norm[:, b * QB:(b + 1) * QB, bass.ds(h * DH, DH)].rearrange("p (c s) j -> p c s j", s=2),
                                        out_t[:, :, :, 0:DH], spread_ap(recip[:, slot], [2, 4], [1, 2], [0, DH]),
                                        ALU.mult).then_inc(unit_scaled[a], 1)

            def shift(i, l):
                if SHIFT_BY[l % QB] == "D":
                    dve.wait_ge(max_done[0], 4 * QB * i + l + 1)
                    t = logit[:, l % NT, :]
                    nc.vector.tensor_scalar(t, t, row_max[:, l % QB:l % QB + 1], None, ALU.subtract).then_inc(shift_dve, 1)

            def pair1(i, first=False):
                for l in range(4 * QB):
                    s, qb = 4 * QB * i + l, l % QB
                    head_slot = l // (2 * QB)
                    if l % (2 * QB) == 0:
                        dve.wait_ge(tab_loaded[head_slot], 16 * (i + 1))
                    dve.wait_ge(sa_done[0], s + 1)
                    if not (first and l < NT):
                        dve.wait_ge(sb_done[0], 2 * (s - NT) + 2)
                    dve.sem_inc(past_wait_dve, 1)
                    tab = bias_tab[:, head_slot, qb * P + L - 1:qb * P + L]
                    bias = bass.AP(tab.tensor, tab.offset, [list(tab.ap[0]), [-1, L]])
                    nc.vector.tensor_tensor_reduce(
                        out=logit[:, l % NT, :], in0=SA[l % 2].rearrange("p a n -> p (a n)"), in1=bias,
                        scale=1.0, scalar=LEAST, op0=ALU.add, op1=ALU.max,
                        accum_out=row_max[:, qb:qb + 1]).then_inc(max_done[0], 1)
                    if l:
                        shift(i, l - 1)
                    if l == 4 * QB - 1:
                        shift(i, l)
                    if qb == 5 and not (first and l < 2 * QB):
                        ul = l // QB
                        scale_unit(0, 4 * i + ul - 2, 2 * i + ul // 2 - 1, ul % 2, ul % 2)

            pair1(0, first=True)
            with dve.Fori(1, PAIRS) as i:
                pair1(i)
            scale_unit(0, U - 2, H - 1, 0, 0)

            def last_units(g):
                if g == G // 2:
                    scale_unit(0, U - 1, H - 1, 1, 1)
                dve.wait_ge(unit_scaled[0], U - 1 if g < G // 2 else U)

            norm_stats(1, norm, last_units)

            def add_x(g, ts):
                nc.vector.tensor_tensor(x_res[:, ts, :], x_res[:, ts, :], norm[:, ts, :], ALU.add).then_inc(x_added[0], 1)

            norm_apply(1, norm, norm, add_x, range(0, G, 2))
            norm_stats(2, x_res, lambda g: dve.wait_ge(x_added[g % 2], g // 2 + 1))
            norm_apply(2, x_res, y_res)
            norm_stats(3, y_res, lambda g: norm_group_out(dve, 2, g))
            norm_apply(3, y_res, norm)
            dve.wait_ge(weights_loaded, 16 * 8)
            feature_major(1, 0)
            projections(1)

            def block_max(u, qb, slot):
                dve.wait_ge(sa_done[1], QB * u + qb + 1)
                nc.vector.tensor_reduce(unit_max[:, slot, qb:qb + 1], SA[qb % 2].rearrange("p a n -> p (a n)"),
                                        AX.X, ALU.max).then_inc(max_done[1], 1)

            def maxima_out(u, slot, stored):
                dve.wait_ge(max_t_mm, u + 1)
                if stored:
                    dve.wait_ge(mrow_stored, 16 * (u - 1))
                nc.vector.tensor_copy(max_rows[:, slot, :], max_t[slot]).then_inc(max_copied, 1)

            for qb in range(QB):
                block_max(0, qb, 0)
            for qb in range(QB):
                block_max(1, qb, 1)
                if qb == MAX_AT:
                    maxima_out(0, 0, False)

            def pair2(i, first=False, last=False):
                for ul in range(4):
                    u = 4 * i + ul
                    for qb in range(QB):
                        if not (last and ul >= 2):
                            block_max(u + AU, qb, ul % 2)
                        if qb == MAX_AT and not (last and ul == 3):
                            maxima_out(u + 1, (ul + 1) % 2, not (first and ul == 0))
                    if not (first and ul == 0):
                        scale_unit(1, u - 1, 2 * i + (ul - 1) // 2, (ul - 1) % 2, (ul - 1) % 2)

            pair2(0, first=True)
            with dve.Fori(1, PAIRS - 1) as i:
                pair2(i)
            pair2(PAIRS - 1, last=True)

            feature_major(2, None, range(G // 2), 2)

            def add_projection(g):
                if g == G // 2:
                    scale_unit(1, U - 1, H - 1, B - 1, B - 1)
                    feature_major(2, None, range(G // 2, G), 2)
                ts = slice(g * TG, (g + 1) * TG)
                dve.wait_ge(proj_mm, g + 1)
                nc.vector.tensor_tensor(y_res[:, ts, :], y_res[:, ts, :],
                                        bank[:, 2 + g, :].rearrange("p (t d) -> p t d", t=TG), ALU.add).then_inc(proj_added, 1)
                dve.wait_ge(proj_added, g + 1)

            norm_stats(4, y_res, add_projection)
            norm_apply(4, y_res, norm)
            feature_major(3, 2, range(G // 2, G), ready=gate_feat_ready)

            n = [0]

            def chain(ins):
                n[0] += 1
                ins.then_inc(gate_step, 1)
                dve.wait_ge(gate_step, n[0])

            dve.wait_ge(moe_consts_ready, 1)
            dve.wait_ge(gate_mm, 1)
            gate_b_all = spread_ap(gate_b_sb[:, :], [0, TT], [1, E])
            order_all = spread_ap(order[:, :], [0, TT], [1, E])
            max_all = spread_ap(gate_max[:, :, :], [1, TT], [0, E])
            hot = onehot[:, 0:TT, :]
            chain(nc.vector.tensor_tensor(gate[:], bank[:, 7, 0:TT * E].rearrange("p (t e) -> p t e", t=TT), gate_b_all, ALU.add))
            chain(nc.vector.tensor_reduce(gate_max[:], gate[:], AX.X, ALU.max))
            chain(nc.vector.tensor_tensor(hot, gate[:], max_all, ALU.is_equal))
            chain(nc.vector.tensor_tensor(gate[:], hot, order_all, ALU.mult))
            chain(nc.vector.tensor_reduce(gate_max[:], gate[:], AX.X, ALU.max))
            chain(nc.vector.tensor_tensor(hot, gate[:], max_all, ALU.is_equal))

            dve.wait_ge(rank_mm, 1)
            rank = bank[:, 6, 0:(TT + 1) * E].rearrange("p (t e) -> p t e", e=E)
            chain(nc.vector.tensor_copy(end_tile[:], rank[:, TT, :].rearrange("p (e o) -> p e o", o=1)))
            chain(nc.vector.tensor_tensor(counts[:], spread_ap(end_tile[:, :, :], [1, E], [0, TT]),
                                          spread_ap(tile_start[:, :], [0, E], [1, TT]), ALU.is_gt))
            chain(nc.vector.tensor_reduce(tiles_of[:], counts[:], AX.X, ALU.add))
            chain(nc.vector.tensor_tensor(pairs_ef[:], lower[:], spread_ap(tiles_of[:, :, :], [0, E], [1, E]), ALU.mult))
            chain(nc.vector.tensor_reduce(first_tile[:], pairs_ef[:], AX.X, ALU.add))
            chain(nc.vector.scalar_tensor_tensor(place[:], spread_ap(first_tile[:, :, :], [0, TT], [1, E]), float(P),
                                                 rank[:, 0:TT, :], ALU.mult, ALU.add))
            chain(nc.vector.tensor_tensor(place[:], place[:], hot, ALU.mult))
            chain(nc.vector.tensor_reduce(slot_f[:], place[:], AX.X, ALU.add))
            slot_by_tile = spread_ap(slot_f[:, :], [1, TT], [0, NS + 1])
            chain(nc.vector.tensor_tensor(at_least[:], slot_by_tile, spread_ap(tile_start[:, :], [0, TT], [1, NS + 1]), ALU.is_ge))
            chain(nc.vector.tensor_reduce(slot_tile[:], at_least[:, :, 1:NS + 1], AX.X, ALU.add))
            chain(nc.vector.scalar_tensor_tensor(place_in_tile[:], slot_tile[:], -float(P), slot_f[:], ALU.mult, ALU.add))
            nc.vector.tensor_tensor(has_place, spread_ap(col_no[:, :], [0, TT], [1, P]),
                                    spread_ap(place_in_tile[:, :], [1, TT], [0, P]), ALU.is_equal).then_inc(numbers_ready, 1)
            chain(nc.vector.tensor_tensor(in_tile[:], at_least[:, :, 0:NS], at_least[:, :, 1:NS + 1], ALU.subtract))
            nc.vector.tensor_scalar(numbers[:, :, 0, :], in_tile[:], row_no[:, 0:1], None, ALU.mult).then_inc(numbers_ready, 1)
            nc.vector.tensor_tensor(numbers[:, :, 1, :], in_tile[:], spread_ap(next_tile_no[:, :], [1, TT], [0, NS]),
                                    ALU.mult).then_inc(numbers_ready, 1)
            dve.wait_ge(numbers_mm, 1)
            chain(nc.vector.tensor_copy(slot_token[:], bank[:, 7, 0:NS]))
            chain(nc.vector.scalar_tensor_tensor(slot_token[:], bank[:, 7, NS:2 * NS], float(P), slot_token[:], ALU.mult, ALU.add))
            nc.vector.tensor_scalar(gather_u[:], slot_token[:], -float(P), 0.0, ALU.add, ALU.max).then_inc(gather_known, 1)
            chain(nc.vector.scalar_tensor_tensor(unused[:], slot_token[:], 0.0, spare_no[:], ALU.is_le, ALU.mult))
            nc.vector.scalar_tensor_tensor(token_u[:], slot_token[:], -float(P), unused[:], ALU.add, ALU.add).then_inc(tokens_known, 1)
            chain(nc.vector.tensor_tensor(end_tile[:], first_tile[:], tiles_of[:], ALU.add))
            chain(nc.vector.tensor_tensor(ended[:], spread_ap(end_tile[:, :, :], [0, NS], [1, E]),
                                          spread_ap(tile_no[:, :], [1, NS], [0, E]), ALU.is_le))
            chain(nc.vector.tensor_reduce(expert_f[:], ended[:], AX.X, ALU.add))
            chain(nc.vector.tensor_scalar(expert_f[:], expert_f[:], float(E - 1), None, ALU.min))
            nc.vector.tensor_copy(expert_u[:], expert_f[:]).then_inc(expert_known, 1)
            dve.wait_ge(expert_known, 1)
            dve.wait_ge(moe_loaded, 16 * (1 + E))

            def weights(i, n, first):
                j = 4 * i + n
                e = dve.value_load(expert_u[0:1, bass.ds(j, 1)], min_val=0, max_val=E - 1)
                if not first:
                    dve.wait_ge(down_mm, j - 3)
                    dve.sem_inc(past_wait_dve, 1)
                nc.vector.tensor_copy(w_ring[:, n, :], w_moe[:, bass.ds(e, 1), :].rearrange("p o w -> p (o w)")).then_inc(w_ready, 1)

            def result(i, n):
                j = 4 * i + n
                dve.wait_ge(down_mm, j + 1)
                dve.sem_inc(past_wait_dve, 1)
                nc.vector.tensor_copy(slot_y[:, bass.ds(j, 1), :].rearrange("p o d -> p (o d)"),
                                      bank[:, 4 + n % 2, 0:D]).then_inc(y_ready, 1)

            def features(i, n):
                j = 4 * i + n
                dve.wait_ge(slot_t_mm, j + 1)
                if not (isinstance(j, int) and j < 4):
                    dve.wait_ge(up_mm, j - 3)
                dve.sem_inc(past_wait_dve, 1)
                nc.vector.tensor_scalar(slot_feat[:, n, :], bank[:, n % 2, 0:P], ln_par[:, 2:3], ln_par[:, 3:4],
                                        ALU.mult, ALU.add).then_inc(slot_t_ready, 1)

            def four_tiles(i, first=False, last=False):
                for n in range(LAST if last else 4):
                    if not (last and n + 1 >= LAST):
                        features(i + (n + 1) // 4, (n + 1) % 4)
                    if not (last and n + 2 >= LAST):
                        weights(i + (n + 2) // 4, (n + 2) % 4, first and n < 2)
                    if n:
                        result(i, n - 1)
                    elif not first:
                        result(i - 1, 3)

            for n in range(2):
                weights(0, n, True)
            features(0, 0)
            four_tiles(0, first=True)
            with dve.Fori(1, BODIES - 1) as i:
                four_tiles(i)
            four_tiles(BODIES - 1, last=True)
            result(BODIES - 1, LAST - 1)

            def add_experts(g):
                ts = slice(g * TG, (g + 1) * TG)
                if g % 2 == 0:
                    dve.wait_ge(y_loaded[g], 16)
                    nc.vector.tensor_tensor(y_res[:, ts, :], y_res[:, ts, :], norm[:, ts, :], ALU.add).then_inc(y_added[0], 1)
                dve.wait_ge(y_added[g % 2], g // 2 + 1)

            norm_stats(5, y_res, add_experts)

            def add_out(g, ts):
                nc.vector.tensor_tensor(norm[:, ts, :], x_res[:, ts, :], norm[:, ts, :], ALU.add).then_inc(out_ready, 1)

            norm_apply(5, y_res, norm, add_out)

        @block.tensor
        def _(pe):
            pe.wait_ge(ident_ready, 1)
            pe.wait_ge(w_in_loaded, 16)
            for c in range(3):
                ins = nc.tensor.transpose(bank[:, 4, c * D:(c + 1) * D], w_in_nat[:, c, :], ident[:])
            ins.then_inc(w_t_mm, 1)

            def keep_warm(n):
                for _ in range(n):
                    nc.tensor.matmul(bank[:, 6, :], ident_b[:], spread_ap(ident_b[:, :], [0, N // P], [1, P]), start=True, stop=True)

            def transposes(a, src, wait):
                for g in range(G):
                    wait(g)
                    for tt in range(TG):
                        ins = nc.tensor.transpose(bank[:, g, tt * P:(tt + 1) * P], src[:, g * TG + tt, :], ident[:])
                    ins.then_inc(tp_done, 1)

            def bias_rows():
                pe.wait_ge(feat_ready, G)
                pe.wait_ge(amp_ready, 1)
                pe.wait_ge(bias_exp, 2)
                for t in range(2):
                    for c in range(4):
                        ins = nc.tensor.matmul(bank[VM * c:VM * (c + 1), 3, :], amp_sel[:, t, :],
                                               bias_e[:, t, c * N:(c + 1) * N],
                                               start=(t == 0), stop=(t == 1), tile_position=(0, VM * c))
                ins.then_inc(bias_mm, 1)

            def projections(a, wq, wk, wv):
                for g in range(G):
                    cols = slice(g * N, (g + 1) * N)
                    pe.wait_ge(feat_ready, a * G + g + 1)
                    if g >= 2:
                        pe.wait_ge(part_rest[a], 2 * g - 3)
                    nc.tensor.matmul(bank[:, 4 + 2 * (g % 2), :], wq, feat[:, cols], start=True, stop=True).then_inc(q_mm[a], 1)
                    if g >= 2:
                        pe.wait_ge(part_rest[a], 2 * g - 2)
                    nc.tensor.matmul(bank[:, 5 + 2 * (g % 2), :], wk, feat[:, cols], start=True, stop=True).then_inc(k_mm[a], 1)
                    if a == 0 and g == G - 1:
                        pe.wait_ge(bias_out, 1)
                    for tt in range(TG):
                        t = g * TG + tt
                        ins = nc.tensor.matmul(bank[:, g, tt * P:(tt + 1) * P], feat[:, t * P:(t + 1) * P], wv,
                                               start=True, stop=True)
                    ins.then_inc(v_mm[a], 1)
                    if a == 0 and g == 1:
                        bias_rows()

            transposes(0, norm, lambda g: norm_group_out(pe, 0, g))
            pe.wait_ge(w_t_ready, 1)
            projections(0, w_in_t[:, 2, :], w_in_t[:, 0, :], w_in_t[:, 1, :])

            def to_natural(a, u, slot, wait, maxima=False):
                pe.wait_ge(o_ready[a], u + 1)
                if wait:
                    pe.wait_ge(unit_scaled[a], u - 1)
                if maxima:
                    pe.wait_ge(max_copied, u + 3)
                for half in range(2):
                    ins = nc.tensor.transpose(AV[slot][:, L // 4 + half * P:L // 4 + (half + 1) * P],
                                              o_ring[:, slot, half * P:(half + 1) * P], ident[:])
                ins.then_inc(unit_t_mm[a], 1)

            def scores_a(slot, head_slot, b, qb, sem_done):
                lhs = q_rows[:, head_slot, b * L + qb * P:b * L + (qb + 1) * P]
                for j in range(2):
                    ins = nc.tensor.matmul(SA[slot][:, j, :], lhs,
                                           k_rows[:, head_slot, b * L + j * N:b * L + (j + 1) * N], start=True, stop=True)
                ins.then_inc(sem_done, 1)

            def weigh_v(a, ul, kb, last_inc):
                head_slot, b = (ul // B) % 2, ul % B
                W = L // 4
                for c in range(4):
                    ins = nc.tensor.matmul(AV[ul % 2][VM * c:VM * (c + 1), 0:W], v_ring[:, head_slot, b * QB + kb, :],
                                           prob[:, ul % 2, kb, c * W:(c + 1) * W], start=(kb == 0), stop=(kb == QB - 1),
                                           tile_position=(0, VM * c))
                if last_inc:
                    ins.then_inc(av_done[a], 1)

            def before_av(a, i, ul, guard_bank):
                u = 4 * i + ul
                if ul % 2 == 0:
                    pe.wait_ge(v_ready[a], 2 * i + ul // 2 + 1)
                if guard_bank:
                    pe.wait_ge(unit_scaled[a], u - 1)

            pe.wait_ge(part_rest[0], 2 * G)
            pe.wait_ge(v_evac[0], G)

            def block_a(i, l, first):
                s = 4 * QB * i + l
                ul, qb = l // QB, l % QB
                if first and l == 0:
                    pe.wait_ge(first_loaded[0], 16 * QK_DMAS)
                elif l % (2 * QB) == (QB if first and l < 2 * QB else 0):
                    pe.wait_ge(qk_loaded[0][(ul // B) % 2], 16 * QK_DMAS * (i + 1 + l // (4 * QB)))
                if not (first and l < 2):
                    pe.wait_ge(max_done[0], s - 1)
                scores_a(l % 2, (ul // B) % 2, ul % B, qb, sa_done[0])

            def pair1(i, first=False, last=False):
                for l in range(4 * QB):
                    ul, qb = l // QB, l % QB
                    pe.wait_ge(shift_sem[SHIFT_BY[qb]], shift_count(i, l))
                    for j in range(2):
                        if not (first and l == 0):
                            pe.wait_ge(exp_done[0], 8 * QB * i + 2 * l + j - 1)
                        for k in range(4):
                            ins = nc.tensor.transpose(SB[j][:, k * P:(k + 1) * P],
                                                      logit[:, l % NT, (4 * j + k) * P:(4 * j + k + 1) * P], ident[:])
                        ins.then_inc(sb_done[0], 1)
                    if not (last and l + 3 >= 4 * QB):
                        block_a(i, l + 3, first)
                    if not (first and ul == 0):
                        if qb == 0:
                            before_av(0, i, ul - 1, not (first and ul < 3))
                            pe.wait_ge(exp_done[0], 2 * QB * (4 * i + ul))
                        weigh_v(0, (ul - 1) % 4, qb, qb == QB - 1)
                    if qb == 2 and not (first and ul < 2):
                        to_natural(0, 4 * i + ul - 2, ul % 2, not (first and ul < 4))

            for l in range(3):
                block_a(0, l, True)
            pair1(0, first=True)
            with pe.Fori(1, PAIRS - 1) as i:
                pair1(i)
            pair1(PAIRS - 1, last=True)
            before_av(0, PAIRS - 1, 3, True)
            pe.wait_ge(exp_done[0], 2 * QB * U)
            for kb in range(QB):
                weigh_v(0, 3, kb, kb == QB - 1)
                if kb == 1:
                    to_natural(0, U - 2, 0, True)

            to_natural(0, U - 1, 1, True)
            pe.wait_ge(unit_scaled[0], U)
            norm_group_out(pe, 2, G - 1)
            keep_warm(WARM)
            transposes(1, norm, lambda g: norm_group_out(pe, 3, g))
            pe.wait_ge(weights_loaded, 16 * 8)
            projections(1, w_qkv_sb[:, 0, :], w_qkv_sb[:, 1, :], w_qkv_sb[:, 2, :])

            pe.wait_ge(part_rest[1], 2 * G)
            pe.wait_ge(v_evac[1], G)

            def block_a2(lu, u, qb, guard, loads=None):
                if loads is not None:
                    pe.wait_ge(qk_loaded[1][(lu // B) % 2], 16 * QK_DMAS * loads)
                if guard:
                    pe.wait_ge(max_done[1], QB * u + qb - 1)
                scores_a(qb % 2, (lu // B) % 2, lu % B, qb, sa_done[1])

            def maxima_t(u, slot, guard):
                pe.wait_ge(split_step, 4 * u + 4)
                if guard:
                    pe.wait_ge(o_ready[1], u - 1)
                nc.tensor.transpose(max_t[slot], max_parts[:, slot, :], ident_b[:]).then_inc(max_t_mm, 1)

            for qb in range(QB):
                if qb == 0:
                    pe.wait_ge(first_loaded[1], 16 * QK_DMAS)
                block_a2(0, 0, qb, qb >= 2)
            pe.wait_ge(qk_loaded[1][0], 16 * QK_DMAS)
            for qb in range(QB):
                block_a2(1, 1, qb, True)
                if qb == MAX_AT:
                    maxima_t(0, 0, False)

            def pair2(i, first=False, last=False):
                for ul in range(4):
                    u, lu = 4 * i + ul, ul + AU
                    head_slot, b = ul // B, ul % B
                    done = last and ul >= 2
                    if b == 0:
                        pe.wait_ge(qkb_loaded[head_slot], 16 * QK_DMAS * (i + 1))
                    pe.wait_ge(mrow_loaded[ul % 2], 16 * (2 * i + ul // 2 + 1))
                    for kb in range(QB):
                        lhs = kb_rows[:, head_slot, b * L + kb * P:b * L + (kb + 1) * P]
                        for half in range(2):
                            if not (first and ul == 0 and kb == 0):
                                pe.wait_ge(exp_done[1], 8 * QB * i + 2 * (QB * ul + kb) + half - 1)
                            nc.tensor.matmul(SB[half], lhs, qb_rows[:, head_slot, b * L + half * N:b * L + (half + 1) * N],
                                             start=True, stop=True).then_inc(sb_done[1], 1)
                        if not done:
                            block_a2(lu, u + AU, kb, True,
                                     i + 1 + lu // 4 if kb == 0 and lu % 2 == 0 else None)
                        if kb == MAX_AT and not (last and ul == 3):
                            maxima_t(u + 1, (ul + 1) % 2, not (first and ul == 0))
                        if kb < 2:
                            if not (first and ul == 0):
                                pe.wait_ge(exp_done[1], 2 * (8 * (4 * i + ul - 1) + kb + 6) + 2)
                                weigh_v(1, (ul - 1) % 4, kb + 6, kb == 1)
                        else:
                            if kb == 2:
                                before_av(1, i, ul, not (first and ul < 2))
                            pe.wait_ge(exp_done[1], 2 * (8 * (4 * i + ul) + kb - 2) + 2)
                            weigh_v(1, ul, kb - 2, False)
                        if kb == 6 and not (first and ul == 0):
                            to_natural(1, u - 1, (ul - 1) % 2, not (first and ul < 3), not (last and ul == 3))

            pair2(0, first=True)
            with pe.Fori(1, PAIRS - 1) as i:
                pair2(i)
            pair2(PAIRS - 1, last=True)

            def output_transposes(groups):
                for g in groups:
                    for tt in range(TG):
                        ins = nc.tensor.transpose(bank[:, g % 2, tt * P:(tt + 1) * P], norm[:, g * TG + tt, :], ident[:])
                    ins.then_inc(tp_done, 1)

            def output_projection(groups):
                for g in groups:
                    pe.wait_ge(feat_ready, 2 * G + g + 1)
                    for tt in range(TG):
                        t = g * TG + tt
                        ins = nc.tensor.matmul(bank[:, 2 + g, tt * P:(tt + 1) * P], feat[:, t * P:(t + 1) * P], w_proj_sb[:],
                                               start=True, stop=True)
                    ins.then_inc(proj_mm, 1)

            pe.wait_ge(unit_scaled[1], U - 1)
            output_transposes(range(G // 2))
            pe.wait_ge(exp_done[1], 2 * QB * U)
            for kb in (6, 7):
                weigh_v(1, 3, kb, kb == 7)
            output_projection(range(G // 2))

            to_natural(1, U - 1, (U - 1) % 2, True)

            pe.wait_ge(unit_scaled[1], U)
            output_transposes(range(G // 2, G))
            output_projection(range(G // 2, G))

            pe.wait_ge(ln_stats, 5 * TT)
            keep_warm(WARM)
            transposes(3, norm, lambda g: norm_group_out(pe, 4, g))
            pe.wait_ge(proj_added, G)
            for t in range(TT):
                g = t // TG
                if g < G // 2:
                    pe.wait_ge(feat_ready, 3 * G + g + 1)
                else:
                    pe.wait_ge(gate_feat_ready, g - G // 2 + 1)
                ins = nc.tensor.matmul(bank[:, 7, t * E:(t + 1) * E], feat[:, t * P:(t + 1) * P], gate_w_sb[:], start=True, stop=True)
            ins.then_inc(gate_mm, 1)
            pe.wait_ge(gate_step, 6)
            out_tiles_e = bank[:, 6, 0:(TT + 1) * E]
            nc.tensor.matmul(out_tiles_e, before[:], onehot[:].rearrange("p t e -> p (t e)"), start=True, stop=False)
            for t in range(TT):
                ins = nc.tensor.matmul(out_tiles_e[:, (t + 1) * E:], ones_b[:], spread_ap(onehot[:, t, :], [0, TT - t], [1, E]),
                                       start=False, stop=(t == TT - 1))
            ins.then_inc(rank_mm, 1)
            pe.wait_ge(numbers_ready, 3)
            for t in range(TT):
                ins = nc.tensor.matmul(bank[:, 7, 0:2 * NS], has_place[:, t, :], numbers[:, t].rearrange("p a j -> p (a j)"),
                                       start=(t == 0), stop=(t == TT - 1))
            ins.then_inc(numbers_mm, 1)

            def sorted_rows(i, n):
                j = 4 * i + n
                pe.wait_ge(slots_loaded[n], 16 * (i + 1))
                if not (isinstance(j, int) and j < 2):
                    pe.wait_ge(slot_t_ready, j - 1)
                nc.tensor.transpose(bank[:, n % 2, 0:P], slot_rows[:, n, :], ident[:]).then_inc(slot_t_mm, 1)

            def up(i, n, first):
                j = 4 * i + n
                pe.wait_ge(w_ready, j + 1)
                pe.wait_ge(slot_t_ready, j + 1)
                if not (first and n < 2):
                    pe.wait_ge(gelu_done, j - 1)
                for c in range(HC):
                    ins = nc.tensor.matmul(bank[:, 2 + n % 2, c * P:(c + 1) * P], w_ring[:, n, c * P:(c + 1) * P],
                                           slot_feat[:, n, :], start=True, stop=True)
                ins.then_inc(up_mm, 1)

            def down(i, n, first):
                j = 4 * i + n
                pe.wait_ge(gelu_done, j + 1)
                if not first:
                    pe.wait_ge(y_ready, j - 1)
                for c in range(HC):
                    ins = nc.tensor.matmul(bank[:, 4 + n % 2, 0:D], hidden[:, n % 2, c, :],
                                           w_ring[:, n, HID + c * D:HID + (c + 1) * D], start=(c == 0), stop=(c == HC - 1))
                ins.then_inc(down_mm, 1)

            def four_tiles(i, first=False, last=False):
                for n in range(LAST if last else 4):
                    if not (last and n + 1 >= LAST):
                        sorted_rows(i + (n + 1) // 4, (n + 1) % 4)
                    up(i, n, first)
                    if n:
                        down(i, n - 1, first and n < 3)
                    elif not first:
                        down(i - 1, 3, False)

            sorted_rows(0, 0)
            four_tiles(0, first=True)
            with pe.Fori(1, BODIES - 1) as i:
                four_tiles(i)
            four_tiles(BODIES - 1, last=True)
            down(BODIES - 1, LAST - 1, False)


_INS = ['L0_attn_x', 'L0_attn_w_in', 'L0_attn_kernel_offsets', 'L0_attn_kernel_amplitudes', 'L0_attn_kernel_sharpness',
        'L0_ffn_ln1_w', 'L0_ffn_ln1_b', 'L0_ffn_w_qkv', 'L0_ffn_w_proj', 'L0_ffn_ln2_w', 'L0_ffn_ln2_b',
        'L0_ffn_gate_w', 'L0_ffn_gate_b', 'L0_ffn_w1', 'L0_ffn_w2']


def kernel(**inputs):
    import numpy as _np
    import concourse.bacc as _bacc
    from concourse import mybir as _mybir
    from concourse.bass_utils import run_bass_kernel_spmd as _run

    nc = _bacc.Bacc("TRN2", target_bir_lowering=False, num_devices=1)
    arrays, args = {}, []
    for name in _INS:
        a = _np.ascontiguousarray(inputs[name])
        arrays[f"in_{name}_dram"] = a
        args.append(nc.dram_tensor(f"in_{name}_dram", a.shape, _mybir.dt.from_np(a.dtype), kind="ExternalInput").ap())
    shape = inputs['L0_attn_x'].shape
    args.append(nc.dram_tensor("out_dram", shape, _mybir.dt.float32, kind="ExternalOutput").ap())
    sandwich_kernel(nc, *args)
    r = _run(nc, [arrays], core_ids=[0])
    return r.results[0]["out_dram"]
```
